# Optimizing a Trainium2 kernel written in Bass

```python
import numpy as np
import jax
import jax.numpy as jnp

def _softmax(x, axis=-1):
    return jax.nn.softmax(x, axis=axis)

def _gelu(x):
    return jax.nn.gelu(x, approximate=True)

def _silu(x):
    return jax.nn.silu(x)

def _sigmoid(x):
    return jax.nn.sigmoid(x)

def _layernorm(x, axis=-1, eps=1e-05):
    m = jnp.mean(x, axis=axis, keepdims=True)
    v = jnp.var(x, axis=axis, keepdims=True)
    return (x - m) / jnp.sqrt(v + eps)

def _scatter_add(tgt, idx, src, axis=0):
    return tgt.at[idx].add(src)

def _segment_sum(src, seg, n):
    return jax.ops.segment_sum(src, seg, n)
kernel_name = 'mk_flamingo_gated_d1_seqx_r4_68bb3c'

def setup_inputs(seed: int=0):
    np.random.seed(seed)
    _w = jnp.asarray

    def _rec_inputs():
        import jax
        import jax.numpy as jnp
        _rk = jax.random.key(seed)
        x = -0.0002928 + 1 * jax.random.normal(jax.random.fold_in(_rk, 1), (16, 112, 512), jnp.float32)
        _lenS = 112 - jax.random.randint(jax.random.fold_in(_rk, 7), (16,), 0, max(1, 112 // 4) + 1, jnp.int32)
        _lenS2 = 375 - jax.random.randint(jax.random.fold_in(_rk, 8), (16,), 0, max(1, 375 // 4) + 1, jnp.int32)
        _ctx_512P = jax.random.normal(jax.random.fold_in(_rk, 11), (16, 16, 128), jnp.float32)
        _ctx_512c = jax.random.dirichlet(jax.random.fold_in(_rk, 511), 0.3 * jnp.ones((16,), jnp.float32), (16, 375))
        _ctx_512t = jnp.einsum('bsk,bkd->bsd', _ctx_512c, _ctx_512P)
        _ctx_512t = _ctx_512t * jax.lax.rsqrt(jnp.mean(jnp.square(_ctx_512t)) + 1e-12) * 0.953939
        ctx_512 = 0.000227908 + 0.99994 * (_ctx_512t + 0.3 * jax.random.normal(jax.random.fold_in(_rk, 611), (16, 375, 128), jnp.float32))
        _g = jax.random.normal(jax.random.fold_in(_rk, 9001), (2, 1), jnp.float32)
        _g = jnp.sign(_g) * jnp.maximum(jnp.abs(_g), 1.0) + (_g == 0) * 1.0
        g_xattn = _g[0]
        g_ffn = _g[1]
        return (x, ctx_512, g_xattn, g_ffn)
    x, ctx_512, g_xattn, g_ffn = _rec_inputs()

    def _L0_xattn_setup():
        import jax, jax.numpy as jnp
        import numpy as np
        B, S, L = (2, 256, 256)
        DIM_Q, H, K, D_C, D_CQ, R = (512, 16, 128, 128, 384, 64)

        def _rope_tables(length, dim):
            inv = 1.0 / 10000.0 ** (jnp.arange(0, dim, 2, dtype=jnp.float32) / dim)
            f = jnp.arange(length, dtype=jnp.float32)[:, None] * inv[None, :]
            sin = jnp.repeat(jnp.sin(f), 2, axis=-1)
            cos = jnp.repeat(jnp.cos(f), 2, axis=-1)
            return (sin, cos)

        def _rotate_half(x):
            half = x.shape[-1] // 2
            return jnp.concatenate([-x[..., half:], x[..., :half]], axis=-1)

        def _apply_rope(x, sin, cos):
            return x * cos + _rotate_half(x) * sin
        key = jax.random.key(seed)
        ks = jax.random.split(key, 8)
        return {'hidden_q': jax.random.normal(ks[0], (B, S, DIM_Q), jnp.float32), 'kv_c': jax.random.normal(ks[1], (B, L, D_C), jnp.float32), 'Wq': jax.random.normal(ks[2], (H * K, DIM_Q), jnp.float32) / np.sqrt(DIM_Q).astype(np.float32), 'w_kc_q': jax.random.normal(ks[3], (H, K, D_CQ), jnp.float32) / np.sqrt(K).astype(np.float32), 'w_kc_kv': jax.random.normal(ks[4], (H, K, D_C), jnp.float32) / np.sqrt(K).astype(np.float32), 'W_qr': jax.random.normal(ks[5], (H, D_CQ, R), jnp.float32) / np.float32(np.sqrt(D_CQ) * np.sqrt(R)), 'W_kr': jax.random.normal(ks[6], (H, D_C, R), jnp.float32) / np.sqrt(D_C).astype(np.float32), 'Wo': jax.random.normal(ks[7], (DIM_Q, H * K), jnp.float32) / np.sqrt(H * K).astype(np.float32)}
    _L0_xattn_all = _L0_xattn_setup()
    _L0_xattn_in = {k: v for k, v in _L0_xattn_all.items() if k in ('Wq', 'w_kc_q', 'w_kc_kv', 'W_qr', 'W_kr', 'Wo')}
    del _L0_xattn_all

    def _L0_ffn_setup():
        import jax, jax.numpy as jnp
        import numpy as np
        H = 512
        E = 64
        I = 128
        SI = 128
        TOP_K = 8
        B, T = (2, 128)
        key = jax.random.key(seed)
        ks = jax.random.split(key, 8)
        s = 0.02
        return {'h': jax.random.normal(ks[0], (B, T, H), jnp.float32), 'gate_w': jax.random.normal(ks[1], (E, H), jnp.float32) * s, 'gu_w': jax.random.normal(ks[2], (E, 2 * I, H), jnp.float32) * s, 'dp_w': jax.random.normal(ks[3], (E, H, I), jnp.float32) * s, 'sh_gate_w': jax.random.normal(ks[4], (SI, H), jnp.float32) * s, 'sh_up_w': jax.random.normal(ks[5], (SI, H), jnp.float32) * s, 'sh_down_w': jax.random.normal(ks[6], (H, SI), jnp.float32) * s, 'sh_gate1_w': jax.random.normal(ks[7], (1, H), jnp.float32) * s}
    _L0_ffn_all = _L0_ffn_setup()
    _L0_ffn_in = {k: v for k, v in _L0_ffn_all.items() if k in ('gate_w', 'gu_w', 'dp_w', 'sh_gate_w', 'sh_up_w', 'sh_down_w', 'sh_gate1_w')}
    del _L0_ffn_all
    return {'x': x, 'ctx_512': ctx_512, 'g_xattn': g_xattn, 'g_ffn': g_ffn, 'L0_xattn_Wq': _L0_xattn_in['Wq'], 'L0_xattn_w_kc_q': _L0_xattn_in['w_kc_q'], 'L0_xattn_w_kc_kv': _L0_xattn_in['w_kc_kv'], 'L0_xattn_W_qr': _L0_xattn_in['W_qr'], 'L0_xattn_W_kr': _L0_xattn_in['W_kr'], 'L0_xattn_Wo': _L0_xattn_in['Wo'], 'L0_ffn_gate_w': _L0_ffn_in['gate_w'], 'L0_ffn_gu_w': _L0_ffn_in['gu_w'], 'L0_ffn_dp_w': _L0_ffn_in['dp_w'], 'L0_ffn_sh_gate_w': _L0_ffn_in['sh_gate_w'], 'L0_ffn_sh_up_w': _L0_ffn_in['sh_up_w'], 'L0_ffn_sh_down_w': _L0_ffn_in['sh_down_w'], 'L0_ffn_sh_gate1_w': _L0_ffn_in['sh_gate1_w']}

def reference(x, ctx_512, g_xattn, g_ffn, L0_xattn_Wq, L0_xattn_w_kc_q, L0_xattn_w_kc_kv, L0_xattn_W_qr, L0_xattn_W_kr, L0_xattn_Wo, L0_ffn_gate_w, L0_ffn_gu_w, L0_ffn_dp_w, L0_ffn_sh_gate_w, L0_ffn_sh_up_w, L0_ffn_sh_down_w, L0_ffn_sh_gate1_w):
    import jax
    import jax.numpy as jnp

    def _L0_xattn_ref(hidden_q, kv_c, Wq, w_kc_q, w_kc_kv, W_qr, W_kr, Wo):
        import jax, jax.numpy as jnp
        import numpy as np
        B, S, L = (2, 256, 256)
        DIM_Q, H, K, D_C, D_CQ, R = (512, 16, 128, 128, 384, 64)

        def _rope_tables(length, dim):
            inv = 1.0 / 10000.0 ** (jnp.arange(0, dim, 2, dtype=jnp.float32) / dim)
            f = jnp.arange(length, dtype=jnp.float32)[:, None] * inv[None, :]
            sin = jnp.repeat(jnp.sin(f), 2, axis=-1)
            cos = jnp.repeat(jnp.cos(f), 2, axis=-1)
            return (sin, cos)

        def _rotate_half(x):
            half = x.shape[-1] // 2
            return jnp.concatenate([-x[..., half:], x[..., :half]], axis=-1)

        def _apply_rope(x, sin, cos):
            return x * cos + _rotate_half(x) * sin
        Bv, Sv, _ = hidden_q.shape
        _, Lv, _ = kv_c.shape
        q_hk = (hidden_q @ Wq.T).reshape(Bv, Sv, H, K)
        q_big = jnp.einsum('bshk,hkq->bshq', q_hk, w_kc_q)
        sin_q, cos_q = _rope_tables(Sv, D_CQ)
        q_big = _apply_rope(q_big, sin_q[None, :, None, :], cos_q[None, :, None, :])
        sin_k, cos_k = _rope_tables(Lv, D_C)
        kv_r = _apply_rope(kv_c, sin_k[None], cos_k[None])
        q_r = jnp.einsum('bshq,hqr->bhsr', q_big, W_qr)
        k_r = jnp.einsum('bld,hdr->bhlr', kv_r, W_kr)
        scores = jnp.einsum('bhsr,bhlr->bhsl', q_r, k_r)
        attn = jax.nn.softmax(scores, axis=-1)
        ctx_c = jnp.einsum('bhsl,bld->bhsd', attn, kv_r)
        ctx_lat = jnp.einsum('bhsd,hkd->bhsk', ctx_c, w_kc_kv)
        ctx = ctx_lat.transpose(0, 2, 1, 3).reshape(Bv, Sv, H * K)
        return ctx @ Wo.T

    def _L0_ffn_ref(h, gate_w, gu_w, dp_w, sh_gate_w, sh_up_w, sh_down_w, sh_gate1_w):
        import jax, jax.numpy as jnp
        import numpy as np
        H = 512
        E = 64
        I = 128
        SI = 128
        TOP_K = 8
        B, T = (2, 128)
        Bb, Tt, Hh = h.shape
        x = h.reshape(Bb * Tt, Hh)
        N = x.shape[0]
        logits = x @ gate_w.T
        topv, topi = jax.lax.top_k(logits, TOP_K)
        rw = jax.nn.softmax(topv.astype(jnp.float32), axis=-1).astype(x.dtype)
        W = jnp.zeros((N, E), x.dtype).at[jnp.arange(N)[:, None], topi].set(rw)
        gu = jnp.einsum('nh,eih->nei', x, gu_w)
        gate, up = (gu[..., :I], gu[..., I:])
        inter = jax.nn.silu(gate) * up
        inter_w = inter * W[:, :, None]
        out = jnp.einsum('nei,ehi->nh', inter_w, dp_w)
        sh_inter = jax.nn.silu(x @ sh_gate_w.T) * (x @ sh_up_w.T)
        sh_out = sh_inter @ sh_down_w.T
        sh_g = jax.nn.sigmoid(x @ sh_gate1_w.T)
        out = out + sh_g * sh_out
        return out.reshape(Bb, Tt, Hh)
    x = x + jnp.tanh(g_xattn[0]) * _L0_xattn_ref(_layernorm(x, axis=-1), ctx_512, L0_xattn_Wq, L0_xattn_w_kc_q, L0_xattn_w_kc_kv, L0_xattn_W_qr, L0_xattn_W_kr, L0_xattn_Wo)
    x = x + jnp.tanh(g_ffn[0]) * _L0_ffn_ref(_layernorm(x, axis=-1), L0_ffn_gate_w, L0_ffn_gu_w, L0_ffn_dp_w, L0_ffn_sh_gate_w, L0_ffn_sh_up_w, L0_ffn_sh_down_w, L0_ffn_sh_gate1_w)
    return x

_drawn_inputs = setup_inputs


def setup_inputs(seed=0):
    import zlib

    import numpy as np

    out = dict(_drawn_inputs(seed))
    spreads = {}
    factors = {'L0_ffn_gate_w': 7.039,
     'L0_ffn_gu_w': 6.315,
     'L0_ffn_dp_w': 6.324,
     'L0_ffn_sh_gate_w': 4.96,
     'L0_ffn_sh_up_w': 4.904,
     'L0_ffn_sh_down_w': 4.897,
     'L0_ffn_sh_gate1_w': 8.0}
    for name, (base, spread) in spreads.items():
        noise = np.random.default_rng([zlib.crc32(name.encode()), seed]).standard_normal(out[name].shape)
        drawn = base * np.exp(spread * noise) if base else spread * noise
        out[name] = jnp.asarray(drawn.astype(out[name].dtype))
    for name, factor in factors.items():
        out[name] = (out[name] * factor).astype(out[name].dtype)
    return out
```

```python
from contextlib import ExitStack

import numpy as np

import concourse.bass as bass
from concourse import mybir

F32 = mybir.dt.float32
I32 = mybir.dt.int32
U32 = mybir.dt.uint32
ALU = mybir.AluOpType
ACT = mybir.ActivationFunctionType
AX_X = mybir.AxisListType.X

B, S, C = 16, 112, 512
L, D = 375, 128
H, K, Q, R = 16, 128, 384, 64
E, I, TOP = 64, 128, 8
EPS = 1e-5

P = 128
CJ = C // P
QJ = Q // P
LJ, LP = 3, L // 3
GB = 4
NG = B // GB
GT = GB * S
ROWS = H * S
RT = ROWS // P

TR = 96
MT = 3
CAP = TR * MT
ROUNDS = -(-(B * S - CAP) // TR)
NT = MT * E + ROUNDS * E
ROUND = 1.5 * 2 ** 23


def rope_tables(length, dim):
    inv = (1.0 / np.float32(10000.0) ** (np.arange(0, dim, 2, dtype=np.float32) / np.float32(dim))).astype(np.float32)
    f = (np.arange(length, dtype=np.float32)[:, None] * inv[None, :]).astype(np.float32)
    sin = np.repeat(np.sin(f), 2, axis=-1).astype(np.float32)
    cos = np.repeat(np.cos(f), 2, axis=-1).astype(np.float32)
    return sin, cos


def shape_constants():
    sq, cq = rope_tables(S, Q)
    sk, ck = rope_tables(L, D)
    half = Q // 2
    sr = np.concatenate([sq[:, half:], -sq[:, :half]], axis=1)
    skn = np.concatenate([-sk[:, :D // 2], sk[:, D // 2:]], axis=1)
    qt = lambda a: np.ascontiguousarray(a.T.reshape(QJ, P, S).transpose(1, 0, 2))
    lt = lambda a: np.ascontiguousarray(a.reshape(LJ, LP, D).transpose(1, 0, 2))
    tri = np.triu(np.ones((S, S), np.float32), 1)
    return {
        "c_cos_q": qt(cq), "c_sin_q": qt(sr), "c_cos_k": lt(ck), "c_sin_k": lt(skn),
        "c_ident": np.eye(P, dtype=np.float32),
        "c_before": tri,
        "c_ones": np.ones((S, P), np.float32),
        "c_expert": np.tile(np.arange(E, dtype=np.float32), (S, 1)),
        "c_token": np.ascontiguousarray(np.arange(B * S, dtype=np.int32).reshape(B, S).T),
        "c_minus_half": np.full((P, 1), -0.5, np.float32),
        "c_table": np.stack([np.repeat(B * S + np.arange(TR, dtype=np.int32)[:, None], NT, axis=1),
                             np.zeros((TR, NT), np.int32)], axis=2),
        "c_pad_rows": np.zeros((TR, C), np.float32),
    }


class Queue:

    def __init__(self, counts):
        self.ops, self.counts, self.passed = [], counts, {}

    def wait(self, *marks):
        for mark in marks:
            if mark is None:
                continue
            sem, value = mark
            if self.passed.get(id(sem), 0) < value:
                self.passed[id(sem)] = value
                self.ops.append(lambda eng, s=sem, v=value: eng.wait_ge(s, v))

    def do(self, fn, sem=None, by=1):
        if sem is None:
            self.ops.append(lambda eng: fn(eng))
            return None
        self.counts[id(sem)] = self.counts.get(id(sem), 0) + by
        self.ops.append(lambda eng: fn(eng).then_inc(sem, by))
        return sem, self.counts[id(sem)]

    def play(self, eng):
        for op in self.ops:
            op(eng)


def build(nc, a, out):
    with ExitStack() as ctx:
        def sb(name, shape, dt=F32):
            return ctx.enter_context(nc.sbuf_tensor(name, shape, dt))

        def sem(name):
            return ctx.enter_context(nc.semaphore(name))

        counts = {}
        pe, dve, act, pool, sp = (Queue(counts) for _ in range(5))

        bank = [ctx.enter_context(nc.psum_tensor(f"bank{i}", [P, 512], F32)) for i in range(8)]
        bank_read = [None] * 8

        m_dram = nc.dram_tensor("m_dram", [H, P, 2 * QJ * D], F32).ap()
        xn2_dram = nc.dram_tensor("xn2_dram", [B * S + TR, C], F32).ap()
        base_dram = nc.dram_tensor("base_dram", [B * S + TR, C], F32).ap()
        table = nc.dram_tensor("table", [TR * NT, 2], I32).ap()
        y_dram = nc.dram_tensor("y_dram", [MT * E * TR, C], F32).ap()

        cos_q = sb("cos_q", [P, QJ, S])
        sin_q = sb("sin_q", [P, QJ, S])
        cos_k = sb("cos_k", [LP, LJ, D])
        sin_k = sb("sin_k", [LP, LJ, D])
        ident = sb("ident", [P, P])
        before = sb("before", [S, S])
        ones = sb("ones", [S, P])
        expert = sb("expert", [S, E])
        token = sb("token", [S, B], I32)
        minus_half = sb("minus_half", [P, 1])
        gates = sb("gates", [P, 2])
        tanh_g = sb("tanh_g", [P, 2])
        router_w = sb("router_w", [P, CJ, E + 1])
        shared_in = sb("shared_in", [P, CJ, 2 * I])
        shared_out = sb("shared_out", [I, C])

        s_const = sem("s_const")
        consts = [(cos_q, a["c_cos_q"]), (sin_q, a["c_sin_q"]), (cos_k, a["c_cos_k"]), (sin_k, a["c_sin_k"]),
                  (ident, a["c_ident"]), (before, a["c_before"]), (ones, a["c_ones"]), (expert, a["c_expert"]),
                  (token, a["c_token"]), (minus_half, a["c_minus_half"]), (router_w, a["router_w"]), (shared_in, a["shared_in"]),
                  (shared_out, a["shared_out"])]
        for dst, src in consts:
            const_loaded = sp.do(lambda e, d=dst, s=src: e.dma_start(d[:], s), s_const, 16)
        for n, g in enumerate((a["g_xattn"], a["g_ffn"])):
            const_loaded = sp.do(lambda e, n=n, g=g: e.dma_start(gates[:, n:n + 1], g.partition_broadcast(P)),
                                 s_const, 16)
        s_zero = sem("s_zero")
        table_3d = table.rearrange("(r t) w -> r t w", r=TR)
        for dst, src in ((table_3d, a["c_table"]), (xn2_dram[B * S:, :], a["c_pad_rows"]),
                         (base_dram[B * S:, :], a["c_pad_rows"])):
            table_clear = sp.do(lambda e, d=dst, s=src: e.dma_start(d, s), s_zero, 16)
        s_tanh = sem("s_tanh")
        act.wait(const_loaded)
        tanh_done = act.do(lambda e: e.activation(tanh_g[:], gates[:], ACT.Tanh), s_tanh)

        v_w = sb("v_w", [D, H, C])
        s_fold_ld = sem("s_fold_ld")
        s_fold = sem("s_fold")
        s_fold_ev = sem("s_fold_ev")
        s_m_st = sem("s_m_st")
        s_v_ld = [sem(f"s_v_ld{i}") for i in range(2)]
        s_v = sem("s_v")
        s_v_ev = sem("s_v_ev")
        with ExitStack() as fold:
            def fsb(name, shape, dt=F32):
                return fold.enter_context(nc.sbuf_tensor(name, shape, dt))

            wqr = fsb("wqr", [R, H, Q])
            wqr_roll = fsb("wqr_roll", [R, H, Q])
            wkr = fsb("wkr", [R, H, D])
            wkv = fsb("wkv", [K, H, D])
            m_sb = fsb("m_sb", [P, 4, 2 * QJ * D])
            wo = fsb("wo", [K, 2, C])
            half = Q // 2
            for dst, src in ((wqr[:], a["w_qr"]), (wkr[:], a["w_kr"]),
                             (wqr_roll[:, :, 0:half], a["w_qr"][:, :, half:Q]),
                             (wqr_roll[:, :, half:Q], a["w_qr"][:, :, 0:half]), (wkv[:], a["w_kv"])):
                fold_loaded = act.do(lambda e, d=dst, s=src: e.dma_start(d, s), s_fold_ld, 16)
            pe.wait(fold_loaded)
            m_stored = []
            s_m_slot = [sem(f"s_m_slot{i}") for i in range(4)]
            for h in range(H):
                b0 = 2 * (h % 4)
                pe.wait(bank_read[b0], bank_read[b0 + 1])
                for j in range(2 * QJ):
                    src = (wqr if j < QJ else wqr_roll)[:, h, (j % QJ) * P:(j % QJ + 1) * P]
                    m_ready = pe.do(lambda e, o=bank[b0 + j // 3][:, (j % 3) * D:(j % 3 + 1) * D], w=src, h=h:
                                    e.matmul(o, w, wkr[:, h, :], start=True, stop=True), s_fold)
                slot = m_sb[:, h % 4, :]
                dve.wait(m_ready, m_stored[h - 4] if h >= 4 else None)
                bank_read[b0] = e0 = dve.do(lambda e, o=slot[:, 0:Q], i=bank[b0][:, 0:Q]: e.tensor_copy(o, i), s_fold_ev)
                act.wait(m_ready, m_stored[h - 4] if h >= 4 else None)
                bank_read[b0 + 1] = e1 = act.do(lambda e, o=slot[:, Q:2 * Q], i=bank[b0 + 1][:, 0:Q]:
                                                e.activation(o, i, ACT.Copy), s_v_ev)
                sp.wait(e0, e1)
                m_stored.append(sp.do(lambda e, h=h, i=slot: e.dma_start(m_dram[h], i), s_m_slot[h % 4], 16))
            v_done = []
            for h in range(H):
                if h >= 2:
                    sp.wait(v_done[h - 2])
                wo_loaded = sp.do(lambda e, h=h: e.dma_start(wo[:, h % 2, :], a["w_o"][h]), s_v_ld[h % 2], 16)
                bk = h % 8
                pe.wait(wo_loaded, bank_read[bk])
                v_done.append(pe.do(lambda e, h=h, bk=bk: e.matmul(bank[bk][:], wkv[:, h, :], wo[:, h % 2, :],
                                                                   start=True, stop=True), s_v))
                act.wait(v_done[-1])
                bank_read[bk] = v_ready = act.do(lambda e, h=h, bk=bk: e.activation(v_w[:, h, :], bank[bk][:], ACT.Copy),
                                                 s_v_ev)
            fold_over = [m_stored[h] for h in range(H - 4, H)] + [v_done[-1]]

        weight = sb("weight", [S, B, TOP])
        slot_i = sb("slot_i", [S, B, TOP], I32)
        count = sb("count", [S, E])
        rounds = sb("rounds", [1, 1], I32)
        kept_sb = sb
        att_ctx = ExitStack()

        def sb(name, shape, dt=F32):
            return att_ctx.enter_context(nc.sbuf_tensor(name, shape, dt))

        NW = 4
        wq = [sb(f"wq{i}", [P, CJ, K]) for i in range(NW)]
        wcq = [sb(f"wcq{i}", [K, Q]) for i in range(NW)]
        m_w = [sb(f"m_w{i}", [P, 2 * QJ, D]) for i in range(NW)]
        xn_t = sb("xn_t", [P, CJ, GB, S])
        q_hk = [sb(f"q_hk{i}", [K, GT]) for i in range(2)]
        q_cos = [sb(f"q_cos{i}", [P, QJ, GT]) for i in range(2)]
        q_sin = [sb(f"q_sin{i}", [P, QJ, GT]) for i in range(2)]
        q_t = sb("q_t", [D, GB, H, S])
        NX = 3
        x_sb = [sb(f"x_sb{i}", [S, C]) for i in range(GB + 1)]
        kv_raw = sb("kv_raw", [LP, LJ, D])
        kv_tmp = sb("kv_tmp", [LP, LJ, D])
        kv_r = [sb(f"kv_r{i}", [LP, LJ, D]) for i in range(2)]
        kv_t = [sb(f"kv_t{i}", [D, L]) for i in range(2)]
        NP = 4
        prob = [sb(f"prob{i}", [P, L]) for i in range(NP)]
        prob_t = [sb(f"prob_t{i}", [LP, LJ, 512]) for i in range(2)]
        row_max = sb("row_max", [P, NP])
        row_sum = sb("row_sum", [P, NP])
        row_inv = sb("row_inv", [P, NP])
        c_t = [sb(f"c_t{i}", [D, ROWS]) for i in range(2)]
        xn1 = sb("xn1", [S, C])
        x2 = sb("x2", [S, C])
        xn2 = sb("xn2", [S, C])
        xn2_t = sb("xn2_t", [P, CJ, S])
        ln_stats = sb("ln_stats", [S, 16])
        logit = sb("logit", [S, E + 1])
        left = sb("left", [S, E])
        mask = sb("mask", [S, E])
        rank_sb = sb("rank_sb", [S, E])
        scratch_e = sb("scratch_e", [S, E])
        top = sb("top", [S, TOP])
        top_i = sb("top_i", [S, TOP], U32)
        pair = sb("pair", [S, 8, TOP])
        pos_i = [sb(f"pos_i{i}", [S, TOP], I32) for i in range(2)]
        entry = [sb(f"entry{i}", [S, TOP, 2], I32) for i in range(2)]
        small = sb("small", [S, 8])
        sh_t = sb("sh_t", [I, S])
        sh_v = sb("sh_v", [I, S])
        sh_w = sb("sh_w", [I, S])
        base = sb("base", [S, C])

        s_x = [sem(f"s_x{i}") for i in range(GB + 1)]
        s_w = [sem(f"s_w{i}") for i in range(NW)]
        s_kv = sem("s_kv")
        s_ln = sem("s_ln")
        s_rstd = sem("s_rstd")
        s_xt = sem("s_xt")
        s_xt_ev = sem("s_xt_ev")
        s_qp = sem("s_qp")
        s_qp_ev = sem("s_qp_ev")
        s_ql = sem("s_ql")
        s_rope = sem("s_rope")
        s_qd = sem("s_qd")
        s_qd_ev = sem("s_qd_ev")
        s_krope = sem("s_krope")
        s_kt = sem("s_kt")
        s_kt_ev = sem("s_kt_ev")
        s_score = sem("s_score")
        s_max = sem("s_max")
        s_exp = sem("s_exp")
        s_norm = sem("s_norm")
        s_pt = sem("s_pt")
        s_pt_ev = sem("s_pt_ev")
        s_ctx = sem("s_ctx")
        s_ctx_ev = sem("s_ctx_ev")
        s_o = sem("s_o")
        s_x2 = sem("s_x2_made")
        s_route = sem("s_route")
        s_sh = sem("s_sh")
        s_sh_a = sem("s_sh_a")
        s_xn2_st = sem("s_xn2_st")
        s_base_st = sem("s_base_st")
        s_tab = [sem(f"s_tab{i}") for i in range(2)]

        x_loaded = [None] * B
        x_used = [None] * B
        xt_ready = [None] * B

        def layer_norm(x_in, x_out, at):
            st, mv, rs = ln_stats[:, at:at + 6], ln_stats[:, at + 6:at + 8], ln_stats[:, at:at + 1]
            dve.wait(dve.do(lambda e: e.bn_stats(st, x_in), s_ln))
            pool.wait(dve.do(lambda e: e.bn_aggr(mv, st), s_ln))
            pool.wait(pool.do(lambda e: e.tensor_scalar(rs, mv[:, 1:2], EPS, None, ALU.add), s_rstd))
            dve.wait(pool.do(lambda e: e.tensor_tensor(rs, rs, minus_half[0:S, :], ALU.pow), s_rstd))
            return dve.do(lambda e: e.tensor_scalar(x_out, x_in, mv[:, 0:1], rs, ALU.subtract, ALU.mult), s_ln)

        def load_x(b):
            if b >= GB + 1:
                sp.wait(x_used[b - GB - 1])
            x_loaded[b] = sp.do(lambda e: e.dma_start(x_sb[b % (GB + 1)][:], a["x"][b * S:(b + 1) * S, :]),
                                s_x[b % (GB + 1)], 16)

        def norm_x(b):
            dve.wait(x_loaded[b], xt_mm[b - 1] if b else None)
            n = layer_norm(x_sb[b % (GB + 1)][:], xn1[:], 0)
            pe.wait(n, bank_read[7])
            for j in range(CJ):
                t = pe.do(lambda e, j=j: e.transpose(bank[7][:, j * S:(j + 1) * S], xn1[:, j * P:(j + 1) * P],
                                                     ident[0:S, 0:S]), s_xt)
            xt_mm[b] = t
            act.wait(t, q_proj_over)
            xt_ready[b] = bank_read[7] = act.do(
                lambda e: e.activation(xn_t[:, :, b % GB, :], bank[7][:, 0:CJ * S].rearrange("p (j s) -> p j s", j=CJ),
                                       ACT.Copy), s_xt_ev)

        xt_mm = [None] * B
        q_proj_over = None

        w_loaded, w_used = [], []

        def load_head(n):
            h, i = n % H, n % NW
            if n >= NW:
                sp.wait(w_used[n - NW])
            else:
                sp.wait(*fold_over)
            for dst, src in ((wq[i][:], a["w_q"][h]), (wcq[i][:], a["w_cq"][h]),
                             (m_w[i][:], m_dram[h].rearrange("p (j d) -> p j d", d=D))):
                mark = sp.do(lambda e, d=dst, s=src: e.dma_start(d, s), s_w[i], 16)
            w_loaded.append(mark)

        def query_phase(g):
            nonlocal q_proj_over
            hk_ready, rope_done, ql_done, qd_done = {}, {}, {}, {}

            def project(h):
                n = g * H + h
                pe.wait(w_loaded[n], bank_read[0], *[xt_ready[g * GB + i] for i in range(GB)])
                for j in range(CJ):
                    m = pe.do(lambda e, j=j: e.matmul(bank[0][:, 0:GT], wq[n % NW][:, j, :],
                                                      xn_t[:, j, :, :].rearrange("p b s -> p (b s)"),
                                                      start=(j == 0), stop=(j == CJ - 1)), s_qp)
                act.wait(m, ql_done.get(h - 2))
                hk_ready[h] = bank_read[0] = act.do(
                    lambda e: e.activation(q_hk[h % 2][:], bank[0][:, 0:GT], ACT.Copy), s_qp_ev)
                return m

            def latent(h):
                n = g * H + h
                for j in range(QJ):
                    pe.wait(hk_ready[h], bank_read[1 + j])
                    m = pe.do(lambda e, j=j: e.matmul(bank[1 + j][:, 0:GT], wcq[n % NW][:, j * P:(j + 1) * P],
                                                      q_hk[h % 2][:], start=True, stop=True), s_ql)
                    dve.wait(m, qd_done.get(h - 2))
                    src = bank[1 + j][:, 0:GT].rearrange("p (b s) -> p b s", b=GB)
                    for dst, tab in ((q_cos, cos_q), (q_sin, sin_q)):
                        r = dve.do(lambda e, d=dst[h % 2], t=tab, j=j, src=src: e.tensor_tensor(
                            d[:, j, :].rearrange("p (b s) -> p b s", b=GB), src,
                            t[:, j, :].unsqueeze(1).to_broadcast([P, GB, S]), ALU.mult), s_rope)
                    bank_read[1 + j] = rope_done[h] = r
                ql_done[h] = m

            def to_context(h):
                n = g * H + h
                pe.wait(rope_done[h], bank_read[4])
                for j in range(2 * QJ):
                    src = (q_cos if j < QJ else q_sin)[h % 2][:, j % QJ, :]
                    m = pe.do(lambda e, j=j, src=src: e.matmul(bank[4][:, 0:GT], m_w[n % NW][:, j, :], src,
                                                               start=(j == 0), stop=(j == 2 * QJ - 1)), s_qd)
                qd_done[h] = m
                w_used.append(m)
                act.wait(m)
                mark = bank_read[4] = act.do(
                    lambda e: e.activation(q_t[:, :, h, :], bank[4][:, 0:GT].rearrange("p (b s) -> p b s", b=GB),
                                           ACT.Copy), s_qd_ev)
                return mark

            for h in range(H + 2):
                if h < H:
                    last = project(h)
                if 1 <= h <= H:
                    latent(h - 1)
                if h >= 2:
                    q_ready = to_context(h - 2)
                if g * H + h + 2 < NG * H and h < H:
                    load_head(g * H + h + 2)
            q_proj_over = last
            return q_ready

        kv_ready = [None] * B
        kvr_ready = [None] * B
        kv_used = [None] * B
        kt_mm = [None] * B
        krope_free = [None]

        def context(b):
            i = b % 2
            sp.wait(krope_free[0])
            loaded = sp.do(lambda e: e.dma_start(kv_raw[:], a["ctx"][b].rearrange("(j p) d -> p j d", p=LP)), s_kv, 16)
            pool.wait(loaded, const_loaded, kv_used[b - 2] if b >= 2 else None)
            hd = D // 2
            pool.do(lambda e: e.tensor_tensor(kv_r[i][:], kv_raw[:], cos_k[:], ALU.mult), s_krope)
            pool.do(lambda e: e.tensor_tensor(kv_tmp[:, :, 0:hd], kv_raw[:, :, hd:D], sin_k[:, :, 0:hd], ALU.mult), s_krope)
            m = pool.do(lambda e: e.tensor_tensor(kv_tmp[:, :, hd:D], kv_raw[:, :, 0:hd], sin_k[:, :, hd:D], ALU.mult),
                        s_krope)
            krope_free[0] = m
            pool.wait(m)
            kvr_ready[b] = pool.do(lambda e: e.tensor_tensor(kv_r[i][:], kv_r[i][:], kv_tmp[:], ALU.add), s_krope)
            pe.wait(kvr_ready[b], bank_read[7])
            for j in range(LJ):
                t = pe.do(lambda e, j=j: e.transpose(bank[7][:, j * LP:(j + 1) * LP], kv_r[i][:, j, :],
                                                     ident[0:LP, 0:LP]), s_kt)
            act.wait(t, scores_over[b - 2] if b >= 2 else None)
            kv_ready[b] = bank_read[7] = act.do(lambda e: e.activation(kv_t[i][:], bank[7][:, 0:L], ACT.Copy), s_kt_ev)

        scores_over = [None] * B
        tile_norm, pt_read = {}, {}
        ctx_mm = {}
        ctx_ev = {}
        NB4 = -(-RT // 4)

        def score_tile(b, t, q_ready):
            n = b * RT + t
            bk, i = n % 3, n % NP
            pe.wait(q_ready, kv_ready[b], bank_read[bk])
            rows = q_t[:, b % GB, :, :].rearrange("d h s -> d (h s)")[:, t * P:(t + 1) * P]
            m = pe.do(lambda e: e.matmul(bank[bk][:, 0:L], rows, kv_t[b % 2][:], start=True, stop=True), s_score)
            scores_over[b] = m
            dve.wait(m, tile_norm.get(n - NP))
            mx = dve.do(lambda e: e.tensor_reduce(row_max[:, i:i + 1], bank[bk][:, 0:L], AX_X, ALU.max, negate=True), s_max)
            act.wait(mx, pt_mm.get(n - NP), tile_norm.get(n - NP))
            ex = bank_read[bk] = act.do(lambda e: e.activation(prob[i][:], bank[bk][:, 0:L], ACT.Exp,
                                                               bias=row_max[:, i:i + 1],
                                                               accum_out=row_sum[:, i:i + 1]), s_exp)
            exp_done[n] = ex

        exp_done, pt_mm = {}, {}

        def normalise(b, t):
            n = b * RT + t
            i = n % NP
            dve.wait(exp_done[n])
            dve.wait(dve.do(lambda e: e.reciprocal(row_inv[:, i:i + 1], row_sum[:, i:i + 1]), s_norm))
            tile_norm[n] = dve.do(lambda e: e.tensor_scalar(prob[i][:], prob[i][:], row_inv[:, i:i + 1], None, ALU.mult),
                                  s_norm)

        def turn_tile(b, t):
            n = b * RT + t
            i, bk = n % NP, 3 + n % 2
            blk = b * NB4 + t // 4
            pe.wait(tile_norm[n], bank_read[bk])
            for j in range(LJ):
                m = pe.do(lambda e, j=j: e.transpose(bank[bk][0:LP, j * P:(j + 1) * P], prob[i][:, j * LP:(j + 1) * LP],
                                                     ident[:]), s_pt)
            pt_mm[n] = m
            src = bank[bk][0:LP, 0:LJ * P].rearrange("p (j r) -> p j r", j=LJ)
            dst = prob_t[blk % 2][:, :, (t % 4) * P:(t % 4 + 1) * P]
            act.wait(m, ctx_mm.get(blk - 2))
            pt_read[n] = bank_read[bk] = act.do(lambda e: e.activation(dst, src, ACT.Copy), s_pt_ev)

        o_mm = {}

        def attend(b, blk4):
            n, width = b * NB4 + blk4, min(4, RT - 4 * blk4) * P
            pe.wait(pt_read[b * RT + min(4 * blk4 + 3, RT - 1)], kvr_ready[b], bank_read[5])
            for j in range(LJ):
                m = pe.do(lambda e, j=j: e.matmul(bank[5][:, 0:width], kv_r[b % 2][:, j, :], prob_t[n % 2][:, j, 0:width],
                                                  start=(j == 0), stop=(j == LJ - 1)), s_ctx)
            ctx_mm[n] = kv_used[b] = m
            dve.wait(m, o_mm.get(b - 2))
            ctx_ev[b] = bank_read[5] = dve.do(
                lambda e: e.tensor_copy(c_t[b % 2][:, blk4 * 512:blk4 * 512 + width], bank[5][:, 0:width]), s_ctx_ev)

        x2_st = [None]
        xn2_stored = [None]

        def project_out(b):
            pe.wait(ctx_ev[b], v_ready, bank_read[6])
            for h in range(H):
                m = pe.do(lambda e, h=h: e.matmul(bank[6][0:S, :], c_t[b % 2][:, h * S:(h + 1) * S], v_w[:, h, :],
                                                  start=(h == 0), stop=(h == H - 1)), s_o)
            o_mm[b] = m
            dve.wait(m, tanh_done, base_done[0], xn2_stored[0], xn2_turned[0])
            r = bank_read[6] = dve.do(lambda e: e.scalar_tensor_tensor(
                x2[:], bank[6][0:S, :], tanh_g[0:S, 0:1], x_sb[b % (GB + 1)][:], ALU.mult, ALU.add), s_x2)
            x_used[b] = r
            dve.wait(r)
            n = layer_norm(x2[:], xn2[:], 8)
            xn2_ready[0] = n
            sp.wait(n)
            xn2_stored[0] = sp.do(lambda e: e.dma_start(xn2_dram[b * S:(b + 1) * S, :], xn2[:]), s_xn2_st, 16)

        base_done, xn2_turned, xn2_ready, xn2t_ready, sh_ready = [None], [None], [None], [None], [None]
        xn2t_used = [None]
        count_used = [None]
        route_done = [None]

        def turn_xn2(b):
            pe.wait(xn2_ready[0], bank_read[7])
            for j in range(CJ):
                m = pe.do(lambda e, j=j: e.transpose(bank[7][:, j * S:(j + 1) * S], xn2[:, j * P:(j + 1) * P],
                                                     ident[0:S, 0:S]), s_xt)
            xn2_turned[0] = m
            act.wait(m, xn2t_used[0])
            xn2t_ready[0] = bank_read[7] = act.do(
                lambda e: e.activation(xn2_t[:], bank[7][:, 0:CJ * S].rearrange("p (j s) -> p j s", j=CJ), ACT.Copy),
                s_xt_ev)

        def router_and_shared_in(b):
            pe.wait(xn2t_ready[0], bank_read[6])
            parts = [(bank[6][0:S, 0:E + 1], lambda j: xn2_t[:, j, :], lambda j: router_w[:, j, :]),
                     (bank[6][:, 128:128 + S], lambda j: shared_in[:, j, 0:I], lambda j: xn2_t[:, j, :]),
                     (bank[6][:, 256:256 + S], lambda j: shared_in[:, j, I:2 * I], lambda j: xn2_t[:, j, :])]
            for o, lhs, rhs in parts:
                for j in range(CJ):
                    m = pe.do(lambda e, o=o, w=lhs(j), x=rhs(j), j=j: e.matmul(o, w, x, start=(j == 0), stop=(j == CJ - 1)),
                              s_sh)
            xn2t_used[0] = m
            gate, up = bank[6][:, 128:128 + S], bank[6][:, 256:256 + S]
            act.wait(m, base_done[0])
            act.do(lambda e: e.activation(sh_t[:], gate, ACT.Tanh, scale=0.5), s_sh_a)
            th = act.do(lambda e: e.activation(small[:, 0:1], bank[6][0:S, E:E + 1], ACT.Tanh, scale=0.5), s_sh_a)
            dve.wait(th, route_done[0])
            dve.do(lambda e: e.tensor_copy(logit[:], bank[6][0:S, 0:E + 1]), s_route)
            v = dve.do(lambda e: e.scalar_tensor_tensor(sh_v[:], sh_t[:], 1.0, gate, ALU.add, ALU.mult), s_route)
            dve.wait(v)
            sh_ready[0] = bank_read[6] = dve.do(
                lambda e: e.scalar_tensor_tensor(sh_w[:], sh_v[:], 0.5, up, ALU.mult, ALU.mult), s_route)

        def shared_down(b):
            pe.wait(sh_ready[0], bank_read[6])
            m = pe.do(lambda e: e.matmul(bank[6][0:S, :], sh_w[:], shared_out[:], start=True, stop=True), s_sh)
            dve.wait(m, base_stored[0])
            dve.wait(dve.do(lambda e: e.tensor_scalar(small[:, 1:2], small[:, 0:1], 1.0, 0.5, ALU.add, ALU.mult), s_route))
            dve.wait(dve.do(lambda e: e.tensor_tensor(small[:, 2:3], small[:, 1:2], tanh_g[0:S, 1:2], ALU.mult), s_route))
            base_done[0] = bank_read[6] = dve.do(lambda e: e.scalar_tensor_tensor(
                base[:], bank[6][0:S, :], small[:, 2:3], x2[:], ALU.mult, ALU.add), s_route)
            sp.wait(base_done[0])
            base_stored[0] = sp.do(lambda e: e.dma_start(base_dram[b * S:(b + 1) * S, :], base[:]), s_base_st, 16)

        base_stored = [None]
        scattered = [None, None]
        count_free = [None]

        def chain(fn):
            mark = dve.do(fn, s_route)
            dve.wait(mark)
            return mark

        def choose(b):
            lg = logit[:, 0:E]
            dve.wait((s_route, counts[id(s_route)]))
            if b == 0:
                dve.do(lambda e: e.memset(count[:], 0.0), s_route)
            chain(lambda e: e.max(top[:], lg))
            dve.do(lambda e: e.max_index(top_i[:], top[:], lg), s_route)
            chain(lambda e: e.match_replace(out=left[:], in_to_replace=top[:], in_values=lg, imm_value=-3.4028235e38))
            if mask_used[0] is not None:
                dve.wait(mask_used[0])
            mk = chain(lambda e: e.tensor_tensor(mask[:], left[:], lg, ALU.not_equal))
            dve.do(lambda e: e.tensor_copy(pair[:, 0, :], top_i[:]), s_route)
            mx = chain(lambda e: e.tensor_scalar(small[:, 3:4], top[:, 0:1], -1.0, None, ALU.mult))
            act.wait(mx)
            ex = act.do(lambda e: e.activation(pair[:, 1, :], top[:], ACT.Exp, bias=small[:, 3:4],
                                               accum_out=small[:, 4:5]), s_sh_a)
            pe.wait(mk, bank_read[7])
            pe.do(lambda e: e.matmul(bank[7][0:S, 0:E], before[:], mask[:], start=True, stop=False), s_sh)
            rank = pe.do(lambda e: e.matmul(bank[7][0:S, 0:E], ones[:, 0:S], count[:], start=False, stop=True), s_sh)
            dve.wait(ex)
            chain(lambda e: e.reciprocal(small[:, 5:6], small[:, 4:5]))
            chain(lambda e: e.tensor_tensor(small[:, 6:7], small[:, 5:6], tanh_g[0:S, 1:2], ALU.mult))
            dve.do(lambda e: e.tensor_scalar(weight[:, b, :], pair[:, 1, :], small[:, 6:7], None, ALU.mult), s_route)
            act.wait(rank, rank_used[0])
            bank_read[7] = act.do(lambda e: e.activation(rank_sb[:], bank[7][0:S, 0:E], ACT.Copy), s_sh_a)
            return bank_read[7]

        mask_used, rank_used = [None], [None]

        def place(b, rank):
            dve.wait(rank)
            for k in range(TOP):
                if k:
                    dve.wait(last)
                last = dve.do(lambda e, k=k: e.scalar_tensor_tensor(
                    scratch_e[:], expert[:], pair[:, 0, k:k + 1], rank_sb[:], ALU.is_equal, ALU.mult,
                    accum_out=pair[:, 2, k:k + 1]), s_route)
            rank_used[0] = last
            dve.wait(last)
            mask_used[0] = dve.do(lambda e: e.tensor_tensor(count[:], count[:], mask[:], ALU.add), s_route)
            ex, r, m, q, t, f, g1 = (pair[:, n, :] for n in (0, 2, 3, 4, 5, 6, 7))
            chain(lambda e: e.tensor_scalar(q, r, -(TR - 1) / 2, 1.0 / TR, ALU.add, ALU.mult))
            chain(lambda e: e.tensor_scalar(q, q, ROUND, -ROUND, ALU.add, ALU.add))
            chain(lambda e: e.scalar_tensor_tensor(m, q, -float(TR), r, ALU.mult, ALU.add))
            chain(lambda e: e.tensor_scalar(f, q, float(MT), None, ALU.is_lt))
            chain(lambda e: e.tensor_scalar(t, q, float(E), None, ALU.mult))
            chain(lambda e: e.tensor_tensor(t, t, ex, ALU.add))
            chain(lambda e: e.tensor_scalar(q, q, float(1 - E), None, ALU.mult))
            chain(lambda e: e.scalar_tensor_tensor(g1, ex, float(MT - 1), q, ALU.mult, ALU.add))
            chain(lambda e: e.tensor_tensor(g1, g1, f, ALU.mult))
            chain(lambda e: e.tensor_tensor(t, t, g1, ALU.add))
            chain(lambda e: e.scalar_tensor_tensor(g1, t, float(TR), m, ALU.mult, ALU.add))
            dve.do(lambda e: e.tensor_tensor(slot_i[:, b, :], g1, f, ALU.mult), s_route)
            dve.wait(scattered[b % 2])
            dve.do(lambda e: e.tensor_copy(entry[b % 2][:, :, 0], token[:, b:b + 1].to_broadcast([S, TOP])), s_route)
            chain(lambda e: e.tensor_copy(entry[b % 2][:, :, 1].bitcast(F32), weight[:, b, :]))
            dve.do(lambda e: e.tensor_tensor(weight[:, b, :], weight[:, b, :], f, ALU.mult), s_route)
            ready = route_done[0] = dve.do(lambda e: e.scalar_tensor_tensor(
                pos_i[b % 2][:], m, float(NT), t, ALU.mult, ALU.add), s_route)
            dve.wait(ready)
            pool.wait(ready, table_clear)
            for k in range(TOP):
                scattered[b % 2] = pool.do(lambda e, k=k: e.indirect_dma_start(
                    table, bass.IndirectOffsetOnAxis(ap=pos_i[b % 2][:, k:k + 1], axis=0), entry[b % 2][:, k, :], None),
                    s_tab[b % 2], 16)

        for queue in (pe, dve, act, pool, sp):
            queue.wait(const_loaded, *fold_over)
        for b in range(GB):
            load_x(b)
        for n in range(2):
            load_head(n)
        for b in range(GB):
            norm_x(b)
        context(0)
        LAG, OUT_LAG = 3, 1
        pending = []
        step = 0
        for g in range(NG):
            q_ready = query_phase(g)
            for t in range(GB * RT + LAG):
                step += 1
                if t >= LAG:
                    b, i = g * GB + (t - LAG) // RT, (t - LAG) % RT
                    turn_tile(b, i)
                    if i % 4 == 3 or i == RT - 1:
                        attend(b, i // 4)
                    if i == RT - 1:
                        project_out(b)
                        pending += [(step + 3, lambda b=b: turn_xn2(b)), (step + 5, lambda b=b: router_and_shared_in(b)),
                                    (step + 7, lambda b=b: shared_down(b)),
                                    (step + 8, lambda b=b: ranks.append(choose(b))),
                                    (step + 9, lambda b=b: place(b, ranks[-1]))]
                if t < GB * RT:
                    b, i = g * GB + t // RT, t % RT
                    score_tile(b, i, q_ready)
                    if i == 7 and b + 1 < B:
                        context(b + 1)
                    if i == 2 and b + GB < B:
                        load_x(b + GB)
                    if i == 11 and b + GB < B:
                        norm_x(b + GB)
                if 1 <= t <= GB * RT:
                    b, i = g * GB + (t - 1) // RT, (t - 1) % RT
                    normalise(b, i)
                if t == 0:
                    ranks = []
                while pending and (pending[0][0] <= step or t == GB * RT + LAG - 1):
                    pending.pop(0)[1]()
        attention_over = [route_done[0], mask_used[0], *scattered, base_stored[0], xn2_stored[0]]
        att_ctx.close()
        sb = kept_sb

        NE = 3
        w_gu = [sb(f"w_gu{i}", [P, CJ, 2 * I]) for i in range(NE)]
        w_dp = [sb(f"w_dp{i}", [I, C]) for i in range(NE)]
        index = sb("index", [TR, MT * E, 2], I32)
        NXG = 3 * MT
        x_g = [sb(f"x_g{i}", [TR, C]) for i in range(NXG)]
        xg_t = [sb(f"xg_t{i}", [P, CJ, CAP]) for i in range(2)]
        e_tanh = [sb(f"e_tanh{i}", [I, CAP]) for i in range(2)]
        e_half = [sb(f"e_half{i}", [I, CAP]) for i in range(2)]
        e_inner = [sb(f"e_inner{i}", [I, CAP]) for i in range(2)]
        NY = 2 * MT
        y_sb = [sb(f"y_sb{i}", [TR, C]) for i in range(NY)]
        total = sb("total", [S, 4])

        s_ew = [sem(f"s_ew{i}") for i in range(NE)]
        s_index = sem("s_index")
        s_xg = [sem(f"s_xg{i}") for i in range(NXG)]
        s_et = sem("s_et")
        s_et_ev = sem("s_et_ev")
        s_gu = sem("s_gu")
        s_tanh_e = sem("s_tanh_e")
        s_inner = sem("s_inner")
        s_down = sem("s_down")
        s_y_a = sem("s_y_a")
        s_y_v = sem("s_y_v")
        s_y_st = [sem(f"s_y_st{i}") for i in range(NY)]
        s_rounds = sem("s_rounds")
        s_loop_over = sem("s_loop_over")

        for queue in (pe, dve, act, pool, sp):
            queue.wait(*attention_over)

        totals = pe.do(lambda e: e.matmul(bank[7][0:S, 0:E], ones[:, 0:S], count[:], start=True, stop=True), s_et)
        dve.wait(totals)
        for fn in (lambda e: e.tensor_reduce(total[:, 0:1], bank[7][0:S, 0:E], AX_X, ALU.max),
                   lambda e: e.tensor_scalar(total[:, 1:2], total[:, 0:1], (TR - 1) / 2 - CAP, 1.0 / TR, ALU.add, ALU.mult),
                   lambda e: e.tensor_scalar(total[:, 2:3], total[:, 1:2], ROUND, -ROUND, ALU.add, ALU.add),
                   lambda e: e.tensor_scalar(total[:, 3:4], total[:, 2:3], 0.0, float(ROUNDS), ALU.max, ALU.min),
                   lambda e: e.tensor_copy(rounds[:], total[0:1, 3:4])):
            rounds_ready = dve.do(fn, s_rounds)
            dve.wait(rounds_ready)
        bank_read[7] = rounds_ready

        index_loaded = sp.do(lambda e: e.dma_start(index[:], table_3d[:, 0:MT * E, :]), s_index, 16)
        ew_loaded, down_done, gathered, turned, gu_done, inner_done = {}, {}, {}, {}, {}, {}
        xt_evacuated, y_stored = {}, {}

        def load_expert(x):
            sp.wait(down_done.get(x - NE))
            for dst, src in ((w_gu[x % NE][:], a["w_gu"][x]), (w_dp[x % NE][:], a["w_dp"][x])):
                ew_loaded[x] = sp.do(lambda e, d=dst, s=src: e.dma_start(d, s), s_ew[x % NE], 16)

        def gather(x):
            pool.wait(index_loaded, turned.get(x - NXG // MT))
            for i in range(MT):
                n = x * MT + i
                gathered[n] = pool.do(lambda e, n=n: e.indirect_dma_start(
                    x_g[n % NXG][:], None, xn2_dram, bass.IndirectOffsetOnAxis(ap=index[:, n, 0:1], axis=0)),
                    s_xg[n % NXG], 16)

        def turn(x):
            for i in range(MT):
                n = x * MT + i
                bk = n % 2
                pe.wait(gathered[n], bank_read[bk])
                for j in range(CJ):
                    m = pe.do(lambda e, n=n, j=j, bk=bk: e.transpose(
                        bank[bk][:, j * TR:(j + 1) * TR], x_g[n % NXG][:, j * P:(j + 1) * P], ident[0:TR, 0:TR]), s_et)
                turned[x] = m
                act.wait(m, gu_done.get(x - 2))
                xt_evacuated[x] = bank_read[bk] = act.do(lambda e, i=i, bk=bk: e.activation(
                    xg_t[x % 2][:, :, i * TR:(i + 1) * TR], bank[bk][:, 0:CJ * TR].rearrange("p (j t) -> p j t", j=CJ),
                    ACT.Copy), s_et_ev)

        def inner(x):
            g, u = 2 + 2 * (x % 2), 3 + 2 * (x % 2)
            pe.wait(ew_loaded[x], xt_evacuated[x], bank_read[g], bank_read[u])
            for bk, at in ((g, 0), (u, I)):
                for j in range(CJ):
                    m = pe.do(lambda e, bk=bk, at=at, j=j: e.matmul(
                        bank[bk][:, 0:CAP], w_gu[x % NE][:, j, at:at + I], xg_t[x % 2][:, j, :],
                        start=(j == 0), stop=(j == CJ - 1)), s_gu)
            gu_done[x] = m
            i = x % 2
            act.wait(m, inner_done.get(x - 2))
            t = act.do(lambda e: e.activation(e_tanh[i][:], bank[g][:, 0:CAP], ACT.Tanh, scale=0.5), s_tanh_e)
            dve.wait(t, down_done.get(x - 2))
            v = dve.do(lambda e: e.scalar_tensor_tensor(e_half[i][:], e_tanh[i][:], 1.0, bank[g][:, 0:CAP], ALU.add,
                                                        ALU.mult), s_inner)
            dve.wait(v)
            inner_done[x] = bank_read[g] = bank_read[u] = dve.do(lambda e: e.scalar_tensor_tensor(
                e_inner[i][:], e_half[i][:], 0.5, bank[u][:, 0:CAP], ALU.mult, ALU.mult), s_inner)

        def down(x):
            for i in range(MT):
                n = x * MT + i
                bk = 6 + n % 2
                pe.wait(ew_loaded[x], inner_done[x], bank_read[bk])
                m = pe.do(lambda e, i=i, bk=bk: e.matmul(bank[bk][0:TR, :], e_inner[x % 2][:, i * TR:(i + 1) * TR],
                                                         w_dp[x % NE][:], start=True, stop=True), s_down)
                down_done[x] = m
                if n % 2:
                    act.wait(m, y_stored.get(n - NY))
                    r = act.do(lambda e, n=n, bk=bk: e.activation(y_sb[n % NY][:], bank[bk][0:TR, :], ACT.Copy), s_y_a)
                else:
                    dve.wait(m, y_stored.get(n - NY))
                    r = dve.do(lambda e, n=n, bk=bk: e.tensor_copy(y_sb[n % NY][:], bank[bk][0:TR, :]), s_y_v)
                bank_read[bk] = r
                sp.wait(r)
                y_stored[n] = sp.do(lambda e, n=n: e.dma_start(y_dram[n * TR:(n + 1) * TR, :], y_sb[n % NY][:]),
                                    s_y_st[n % NY], 16)

        for x in range(2):
            load_expert(x)
            gather(x)
        turn(0)
        for x in range(E + 1):
            if x + 1 < E:
                turn(x + 1)
            if x < E:
                inner(x)
            if x >= 1:
                down(x - 1)
            if x + 2 < E:
                load_expert(x + 2)
                gather(x + 2)
        stores = [y_stored[n] for n in range(MT * E - NY, MT * E)]

        lp = {n: sem(f"s_loop_{n}") for n in ("load", "gather", "turn", "turned", "gu", "tanh", "half", "inner", "down",
                                              "y", "stored")}
        s_loop_gather = sem("s_loop_gather_dma")
        s_loop_add = sem("s_loop_add_dma")
        l_index = sb("l_index", [TR, 2], I32)

        def take(eng, name, value=1):
            eng.wait_ge(lp[name], value)
            eng.sem_clear(lp[name])

        def loop(body):
            def run(eng):
                n = eng.value_load(rounds[0:1, 0:1], min_val=0, max_val=ROUNDS)
                with eng.If(n > 0):
                    with eng.Fori(0, n) as r:
                        with eng.Fori(0, E) as x:
                            body(eng, r, x)
            return run

        def loop_sp(eng, r, x):
            tile = (r + MT) * E + x
            eng.dma_start(w_gu[0][:], a["w_gu"][bass.ds(x, 1)].rearrange("one p j i -> p (one j) i")).then_inc(lp["load"], 16)
            eng.dma_start(w_dp[0][:], a["w_dp"][bass.ds(x, 1)].rearrange("one i c -> i (one c)")).then_inc(lp["load"], 16)
            eng.dma_start(l_index[:], table_3d[:, bass.ds(tile, 1), :].rearrange("r one w -> r (one w)")).then_inc(lp["load"], 16)
            take(eng, "stored")

        def loop_pool(eng, r, x):
            take(eng, "load", 48)
            eng.indirect_dma_start(x_g[0][:], None, xn2_dram, bass.IndirectOffsetOnAxis(ap=l_index[:, 0:1], axis=0))\
               .then_inc(s_loop_gather, 16)
            eng.wait_ge(s_loop_gather, (r * E + x + 1) * 16)
            eng.nop().then_inc(lp["gather"], 1)
            take(eng, "y")
            eng.indirect_dma_start(base_dram, bass.IndirectOffsetOnAxis(ap=l_index[:, 0:1], axis=0), y_sb[0][:], None,
                                   compute_op=ALU.add).then_inc(s_loop_add, 16)
            eng.wait_ge(s_loop_add, (r * E + x + 1) * 16)
            eng.nop().then_inc(lp["stored"], 1)

        def loop_pe(eng, r, x):
            take(eng, "gather")
            for j in range(CJ):
                m = eng.transpose(bank[0][:, j * TR:(j + 1) * TR], x_g[0][:, j * P:(j + 1) * P], ident[0:TR, 0:TR])
            m.then_inc(lp["turn"], 1)
            take(eng, "turned")
            for bk, at in ((2, 0), (3, I)):
                for j in range(CJ):
                    m = eng.matmul(bank[bk][:, 0:TR], w_gu[0][:, j, at:at + I], xg_t[0][:, j, 0:TR],
                                   start=(j == 0), stop=(j == CJ - 1))
            m.then_inc(lp["gu"], 1)
            take(eng, "inner")
            eng.matmul(bank[6][0:TR, :], e_inner[0][:, 0:TR], w_dp[0][:], start=True, stop=True).then_inc(lp["down"], 1)

        def loop_act(eng, r, x):
            take(eng, "turn")
            eng.activation(xg_t[0][:, :, 0:TR], bank[0][:, 0:CJ * TR].rearrange("p (j t) -> p j t", j=CJ), ACT.Copy)\
               .then_inc(lp["turned"], 1)
            take(eng, "gu")
            eng.activation(e_tanh[0][:, 0:TR], bank[2][:, 0:TR], ACT.Tanh, scale=0.5).then_inc(lp["tanh"], 1)
            take(eng, "down")
            eng.activation(y_sb[0][:], bank[6][0:TR, :], ACT.Copy, scale=l_index[:, 1:2].bitcast(F32)).then_inc(lp["y"], 1)

        def loop_dve(eng, r, x):
            take(eng, "tanh")
            eng.scalar_tensor_tensor(e_half[0][:, 0:TR], e_tanh[0][:, 0:TR], 1.0, bank[2][:, 0:TR], ALU.add,
                                     ALU.mult).then_inc(lp["half"], 1)
            take(eng, "half")
            eng.scalar_tensor_tensor(e_inner[0][:, 0:TR], e_half[0][:, 0:TR], 0.5, bank[3][:, 0:TR], ALU.mult,
                                     ALU.mult).then_inc(lp["inner"], 1)

        for queue, body in ((sp, loop_sp), (pool, loop_pool), (pe, loop_pe), (act, loop_act), (dve, loop_dve)):
            queue.wait(rounds_ready, *stores)
            queue.ops.append(loop(body))
        loop_over = sp.do(lambda e: e.nop(), s_loop_over)

        NG8 = 2 * TOP
        y_g = [sb(f"y_g{i}", [S, C]) for i in range(NG8)]
        acc = [sb(f"acc{i}", [S, C]) for i in range(3)]
        s_yg = [sem(f"s_yg{i}") for i in range(NG8)]
        s_base_ld = [sem(f"s_base_ld{i}") for i in range(3)]
        s_acc = sem("s_acc")
        s_out = [sem(f"s_out{i}") for i in range(3)]
        pool.wait(loop_over)
        added, out_stored, base_loaded = {}, {}, {}
        for b in range(B):
            sp.wait(out_stored.get(b - 3))
            base_loaded[b] = sp.do(lambda e, b=b: e.dma_start(acc[b % 3][:], base_dram[b * S:(b + 1) * S, :]),
                                   s_base_ld[b % 3], 16)
            dve.wait(base_loaded[b])
            for k in range(TOP):
                n = b * TOP + k
                pool.wait(added.get(n - NG8))
                got = pool.do(lambda e, n=n, b=b, k=k: e.indirect_dma_start(
                    y_g[n % NG8][:], None, y_dram, bass.IndirectOffsetOnAxis(ap=slot_i[:, b, k:k + 1], axis=0)),
                    s_yg[n % NG8], 16)
                dve.wait(got, added.get(n - 1))
                added[n] = dve.do(lambda e, n=n, b=b, k=k: e.scalar_tensor_tensor(
                    acc[b % 3][:], y_g[n % NG8][:], weight[:, b, k:k + 1], acc[b % 3][:], ALU.mult, ALU.add), s_acc)
            if b >= 1:
                out_stored[b - 1] = store_out(sp, added[b * TOP - 1], out, acc, b - 1, s_out)
        out_stored[B - 1] = store_out(sp, added[B * TOP - 1], out, acc, B - 1, s_out)
        sp.wait(*[out_stored[b] for b in range(B - 3, B)])

        block = ctx.enter_context(nc.Block())
        block.sync(sp.play)
        block.tensor(pe.play)
        block.vector(dve.play)
        block.scalar(act.play)
        block.gpsimd(pool.play)


def store_out(sp, ready, out, acc, b, s_out):
    sp.wait(ready)
    return sp.do(lambda e: e.dma_start(out[b * S:(b + 1) * S, :], acc[b % 3][:]), s_out[b % 3], 16)


_OUT = ((B, S, C), "float32")


def lay_out(x, ctx_512, g_xattn, g_ffn, L0_xattn_Wq, L0_xattn_w_kc_q, L0_xattn_w_kc_kv, L0_xattn_W_qr, L0_xattn_W_kr,
            L0_xattn_Wo, L0_ffn_gate_w, L0_ffn_gu_w, L0_ffn_dp_w, L0_ffn_sh_gate_w, L0_ffn_sh_up_w, L0_ffn_sh_down_w,
            L0_ffn_sh_gate1_w):
    cut = lambda w: np.asarray(w).T.reshape(CJ, P, -1).transpose(1, 0, 2)
    arrays = {
        "x": np.asarray(x).reshape(B * S, C),
        "ctx": np.asarray(ctx_512),
        "g_xattn": np.asarray(g_xattn), "g_ffn": np.asarray(g_ffn),
        "w_q": np.asarray(L0_xattn_Wq).reshape(H, K, CJ, P).transpose(0, 3, 2, 1),
        "w_cq": np.asarray(L0_xattn_w_kc_q),
        "w_qr": np.asarray(L0_xattn_W_qr).transpose(2, 0, 1),
        "w_kr": np.asarray(L0_xattn_W_kr).transpose(2, 0, 1),
        "w_kv": np.asarray(L0_xattn_w_kc_kv).transpose(1, 0, 2),
        "w_o": np.asarray(L0_xattn_Wo).reshape(C, H, K).transpose(1, 2, 0),
        "router_w": cut(np.concatenate([np.asarray(L0_ffn_gate_w), np.asarray(L0_ffn_sh_gate1_w)])),
        "shared_in": cut(np.concatenate([np.asarray(L0_ffn_sh_gate_w), np.asarray(L0_ffn_sh_up_w)])),
        "shared_out": np.asarray(L0_ffn_sh_down_w).T,
        "w_gu": np.asarray(L0_ffn_gu_w).reshape(E, 2 * I, CJ, P).transpose(0, 3, 2, 1),
        "w_dp": np.asarray(L0_ffn_dp_w).transpose(0, 2, 1),
    }
    arrays.update(shape_constants())
    return {k: np.ascontiguousarray(v) for k, v in arrays.items()}


def kernel(**inputs):
    import concourse.bacc as _bacc
    from concourse.bass_utils import run_bass_kernel_spmd as _run

    nc = _bacc.Bacc("TRN2", target_bir_lowering=False, num_devices=1)
    arrays = lay_out(**inputs)
    aps = {n: nc.dram_tensor(f"in_{n}", v.shape, mybir.dt.from_np(v.dtype), kind="ExternalInput").ap()
           for n, v in arrays.items()}
    out = nc.dram_tensor("out", [B * S, C], F32, kind="ExternalOutput").ap()
    build(nc, aps, out)
    r = _run(nc, [{f"in_{n}": v for n, v in arrays.items()}], core_ids=[0])
    return np.asarray(r.results[0]["out"]).reshape(_OUT[0])
```

```python
from contextlib import ExitStack

import numpy as np

import concourse.bass as bass
from concourse import mybir

F32 = mybir.dt.float32
F32R = mybir.dt.float32r
I32 = mybir.dt.int32
U32 = mybir.dt.uint32
ALU = mybir.AluOpType
ACT = mybir.ActivationFunctionType
AX_X = mybir.AxisListType.X

B, S, C = 16, 112, 512
L, D = 375, 128
H, K, Q, R = 16, 128, 384, 64
E, I, TOP = 64, 128, 8
EPS = 1e-5

P = 128
CJ = C // P
QC = 4
QW = Q // QC
LJ, LP = 3, L // 3
GB = 4
NG = B // GB
GT = GB * S
ROWS = H * S
RT = ROWS // P

TR = 96
MT = 3
CAP = TR * MT
ROUNDS = -(-(B * S - CAP) // TR)
NT = MT * E + ROUNDS * E
ROUND = 1.5 * 2 ** 23


def rope_tables(length, dim):
    inv = (1.0 / np.float32(10000.0) ** (np.arange(0, dim, 2, dtype=np.float32) / np.float32(dim))).astype(np.float32)
    f = (np.arange(length, dtype=np.float32)[:, None] * inv[None, :]).astype(np.float32)
    sin = np.repeat(np.sin(f), 2, axis=-1).astype(np.float32)
    cos = np.repeat(np.cos(f), 2, axis=-1).astype(np.float32)
    return sin, cos


def shape_constants():
    sq, cq = rope_tables(S, Q)
    sk, ck = rope_tables(L, D)
    half = Q // 2
    sr = np.concatenate([-sq[:, :half], sq[:, half:]], axis=1)
    skn = np.concatenate([-sk[:, :D // 2], sk[:, D // 2:]], axis=1)
    qt = lambda a: np.ascontiguousarray(a.T.reshape(QC, QW, S).transpose(1, 0, 2))
    lt = lambda a: np.ascontiguousarray(a.reshape(LJ, LP, D).transpose(1, 0, 2))
    tri = np.triu(np.ones((S, S), np.float32), 1)
    return {
        "c_cos_q": qt(cq), "c_sin_q": qt(sr), "c_cos_k": lt(ck), "c_sin_k": lt(skn),
        "c_ident": np.eye(P, dtype=np.float32),
        "c_before": tri,
        "c_ones": np.ones((S, P), np.float32),
        "c_expert": np.tile(np.arange(E, dtype=np.float32), (S, 1)),
        "c_token": np.ascontiguousarray(np.arange(B * S, dtype=np.int32).reshape(B, S).T),
        "c_minus_half": np.full((P, 1), -0.5, np.float32),
        "c_table": np.stack([B * S + np.arange(TR, dtype=np.int32)[:, None]
                             + TR * (np.arange(NT, dtype=np.int32)[None, :] % MT),
                             np.zeros((TR, NT), np.int32)], axis=2),
        "c_pad_rows": np.zeros((CAP, C), np.float32),
    }


class Queue:

    def __init__(self, counts):
        self.ops, self.counts, self.passed = [], counts, {}

    def wait(self, *marks):
        for mark in marks:
            if mark is None:
                continue
            sem, value = mark
            if self.passed.get(id(sem), 0) < value:
                self.passed[id(sem)] = value
                self.ops.append(lambda eng, s=sem, v=value: eng.wait_ge(s, v))

    def do(self, fn, sem=None, by=1):
        if sem is None:
            self.ops.append(lambda eng: fn(eng))
            return None
        self.counts[id(sem)] = self.counts.get(id(sem), 0) + by
        self.ops.append(lambda eng: fn(eng).then_inc(sem, by))
        return sem, self.counts[id(sem)]

    def play(self, eng):
        for op in self.ops:
            op(eng)


def build(nc, a, out):
    with ExitStack() as ctx:
        def sb(name, shape, dt=F32):
            return ctx.enter_context(nc.sbuf_tensor(name, shape, dt))

        def sem(name):
            return ctx.enter_context(nc.semaphore(name))

        counts = {}
        pe, dve, act, pool, sp = (Queue(counts) for _ in range(5))

        bank = [ctx.enter_context(nc.psum_tensor(f"bank{i}", [P, 512], F32)) for i in range(8)]
        bank_read = [None] * 8

        m_dram = nc.dram_tensor("m_dram", [H, QW, QC * D], F32).ap()
        v_dram = nc.dram_tensor("v_dram", [H, D, C], F32).ap()
        xn2_dram = nc.dram_tensor("xn2_dram", [B * S + CAP, C], F32).ap()
        table = nc.dram_tensor("table", [TR * NT, 2], I32).ap()

        cos_q = sb("cos_q", [QW, QC, S])
        sin_q = sb("sin_q", [QW, QC, S])
        cos_k = sb("cos_k", [LP, LJ, D])
        sin_k = sb("sin_k", [LP, LJ, D])
        ident = sb("ident", [P, P])
        before = sb("before", [S, S])
        ones = sb("ones", [S, P])
        expert = sb("expert", [S, E])
        token = sb("token", [S, B], I32)
        minus_half = sb("minus_half", [P, 1])
        gates = sb("gates", [P, 2])
        tanh_g = sb("tanh_g", [P, 2])
        router_w = sb("router_w", [P, CJ, E + 1])
        shared_in = sb("shared_in", [P, CJ, 2 * I])
        shared_out = sb("shared_out", [I, C])

        s_const = sem("s_const")
        consts = [(cos_q, a["c_cos_q"]), (sin_q, a["c_sin_q"]), (cos_k, a["c_cos_k"]), (sin_k, a["c_sin_k"]),
                  (ident, a["c_ident"]), (before, a["c_before"]), (ones, a["c_ones"]), (expert, a["c_expert"]),
                  (token, a["c_token"]), (minus_half, a["c_minus_half"]), (router_w, a["router_w"]), (shared_in, a["shared_in"]),
                  (shared_out, a["shared_out"])]
        for dst, src in consts:
            const_loaded = sp.do(lambda e, d=dst, s=src: e.dma_start(d[:], s), s_const, 16)
        for n, g in enumerate((a["g_xattn"], a["g_ffn"])):
            const_loaded = sp.do(lambda e, n=n, g=g: e.dma_start(gates[:, n:n + 1], g.partition_broadcast(P)),
                                 s_const, 16)
        s_zero = sem("s_zero")
        s_pad = sem("s_pad")
        dve.wait(const_loaded)
        table_3d = table.rearrange("(r t) w -> r t w", r=TR)
        for dst, src in ((table_3d, a["c_table"]), (xn2_dram[B * S:, :], a["c_pad_rows"]),
                         (out[B * S:, :], a["c_pad_rows"])):
            table_clear = sp.do(lambda e, d=dst, s=src: e.dma_start(d, s), s_zero, 16)
        s_tanh = sem("s_tanh")
        act.wait(const_loaded)
        tanh_done = act.do(lambda e: e.activation(tanh_g[:], gates[:], ACT.Tanh), s_tanh)

        def fold_weights():
            s_fold_qr = sem("s_fold_qr")
            s_fold_kv = sem("s_fold_kv")
            s_fold = sem("s_fold")
            s_fold_v = sem("s_fold_v")
            s_fold_a = sem("s_fold_a")
            s_m_st = [sem(f"s_m_st{i}") for i in range(NF)]
            s_v_ld = [sem(f"s_v_ld{i}") for i in range(NF)]
            s_v_st = [sem(f"s_v_st{i}") for i in range(NF)]
            for dst, src in ((wqr[:], a["w_qr"]), (wkr[:], a["w_kr"])):
                qr_loaded = act.do(lambda e, d=dst, s=src: e.dma_start(d, s), s_fold_qr, 16)
            kv_loaded = act.do(lambda e: e.dma_start(wkv[:], a["w_kv"]), s_fold_kv, 16)
            pe.wait(qr_loaded)
            for h in range(H):
                bk = h % 8
                pe.wait(bank_read[bk])
                for c in range(QC):
                    m_ready = pe.do(lambda e, h=h, c=c, bk=bk: e.matmul(
                        bank[bk][0:QW, c * D:(c + 1) * D], wqr[:, h, c * QW:(c + 1) * QW], wkr[:, h, :],
                        start=True, stop=True), s_fold)
                (dve if h % 2 else act).wait(m_ready, m_stored[h - NF] if h >= NF else None)
                slot = m_sb[:, h % NF, :]
                if h % 2:
                    done = dve.do(lambda e, bk=bk, o=slot: e.tensor_copy(o, bank[bk][0:QW, :]), s_fold_v)
                else:
                    done = act.do(lambda e, bk=bk, o=slot: e.activation(o, bank[bk][0:QW, :], ACT.Copy), s_fold_a)
                bank_read[bk] = done
                sp.wait(done)
                m_stored.append(sp.do(lambda e, h=h, i=slot: e.dma_start(m_dram[h], i), s_m_st[h % NF], 16))
            v_done = []
            pe.wait(kv_loaded)
            for h in range(H):
                sp.wait(v_done[h - NF] if h >= NF else None)
                wo_loaded = sp.do(lambda e, h=h: e.dma_start(wo[:, h % NF, :], a["w_o"][h]), s_v_ld[h % NF], 16)
                bk = h % 8
                pe.wait(wo_loaded, bank_read[bk])
                v_done.append(pe.do(lambda e, h=h, bk=bk: e.matmul(bank[bk][:], wkv[:, h, :], wo[:, h % NF, :],
                                                                   start=True, stop=True), s_fold))
                slot = v_sb[h % NF]
                act.wait(v_done[-1], v_stored[h - NF] if h >= NF else None)
                bank_read[bk] = copied = act.do(lambda e, bk=bk, o=slot: e.activation(o[:], bank[bk][:], ACT.Copy), s_fold_a)
                act.wait(copied)
                v_stored.append(act.do(lambda e, h=h, i=slot: e.dma_start(v_dram[h], i[:]), s_v_st[h % NF], 16))
            return [*m_stored[-NF:], *v_stored[-NF:]]

        m_stored, v_stored = [], []
        NF = 3

        count = sb("count", [S, E])
        rounds = sb("rounds", [1, 1], I32)
        kept_sb = sb
        att_ctx = ExitStack()

        def sb(name, shape, dt=F32):
            return att_ctx.enter_context(nc.sbuf_tensor(name, shape, dt))

        NW = 2
        wq = [sb(f"wq{i}", [P, CJ, K]) for i in range(NW)]
        wcq = [sb(f"wcq{i}", [K, Q]) for i in range(NW)]
        m_w = [sb(f"m_w{i}", [QW, QC, D]) for i in range(NW)]
        wq_s = [[sb(f"wq_s{i}{p}", [P, CJ, K], F32R) for p in "hl"] for i in range(2)]
        wcq_s = [[sb(f"wcq_s{i}{p}", [K, Q], F32R) for p in "hl"] for i in range(2)]
        NV = 2
        v_raw = [sb(f"v_raw{i}", [D, C]) for i in range(NV)]
        v_w = [[sb(f"v_w{i}{p}", [D, C], F32R) for p in "hl"] for i in range(NV)]
        xn_t = [sb(f"xn_t{p}", [P, CJ, GB, S], F32R) for p in "hl"]
        NX = 2 * GB
        x_sb = [sb(f"x_sb{i}", [S, C]) for i in range(NX)]
        kv_raw = sb("kv_raw", [LP, LJ, D])
        kv_tmp = sb("kv_tmp", [LP, LJ, D])
        kv_full = sb("kv_full", [LP, LJ, D])
        kv_r = [[sb(f"kv_r{i}{p}", [LP, LJ, D], F32R) for p in "hl"] for i in range(2)]
        kv_t = [[sb(f"kv_t{i}{p}", [D, L + 1], F32R) for p in "hl"] for i in range(2)]
        for part in (*kv_t[0], *kv_t[1]):
            dve.do(lambda e, o=part: e.tensor_scalar(o[:, L:L + 1], ident[:, 0:1], 0.0, None, ALU.mult), s_pad)
        NP = 4
        row_max = sb("row_max", [P, NP])
        row_sum = sb("row_sum", [P, NP])
        row_inv = sb("row_inv", [P, NP])
        xn1 = sb("xn1", [S, C])
        xn2 = sb("xn2", [S, C])
        xn2_t = sb("xn2_t", [P, CJ, S])
        ln_stats = [sb(f"ln_stats{i}", [S, 16]) for i in range(GB + 1)]
        logit = sb("logit", [S, E + 1])
        left = sb("left", [S, E])
        mask = sb("mask", [S, E])
        rank_sb = sb("rank_sb", [S, E])
        scratch_e = sb("scratch_e", [S, E])
        top = sb("top", [S, TOP])
        top_i = sb("top_i", [S, TOP], U32)
        pair = sb("pair", [S, 8, TOP])
        weight = [sb(f"weight{i}", [S, TOP]) for i in range(2)]
        pos_i = [sb(f"pos_i{i}", [S, TOP], I32) for i in range(2)]
        entry = [sb(f"entry{i}", [S, TOP, 2], I32) for i in range(2)]
        small = sb("small", [S, 8])
        sh_t = sb("sh_t", [I, S])
        sh_v = sb("sh_v", [I, S])
        sh_w = sb("sh_w", [I, S])
        with ExitStack() as turn_ctx:
            def turn_sb(name, shape, dt=F32):
                return turn_ctx.enter_context(nc.sbuf_tensor(name, shape, dt))

            q_hk = [[turn_sb(f"q_hk{i}{p}", [K, GT], F32R) for p in "hl"] for i in range(2)]
            q_rope = [turn_sb(f"q_rope{i}", [QW, QC, GT]) for i in range(2)]
            q_sin = turn_sb("q_sin", [QW, QC, GT])
        prob = [sb(f"prob{i}", [P, L]) for i in range(NP)]
        TB = 4
        prob_t = [[sb(f"prob_t{i}{p}", [LP, LJ, TB * P], F32R) for p in "hl"] for i in range(2)]
        with ExitStack() as fold:
            def fsb(name, shape, dt=F32):
                return fold.enter_context(nc.sbuf_tensor(name, shape, dt))

            wqr = fsb("wqr", [R, H, Q])
            wkr = fsb("wkr", [R, H, D])
            wkv = fsb("wkv", [K, H, D])
            m_sb = fsb("m_sb", [QW, NF, QC * D])
            wo = fsb("wo", [K, NF, C])
            v_sb = [fsb(f"v_sb{i}", [D, C]) for i in range(NF)]
        q_t = [sb(f"q_t{p}", [D, GB, H, S], F32R) for p in "hl"]

        s_x = [sem(f"s_x{i}") for i in range(NX)]
        s_w = {kind: [sem(f"s_{kind}{i}") for i in range(NW)] for kind in ("wq", "wcq", "m_w")}
        s_vl = [sem(f"s_vl{i}") for i in range(NV)]
        s_v_high = sem("s_v_high")
        s_v_low = sem("s_v_low")
        s_kv = sem("s_kv")
        s_ln = sem("s_ln")
        s_rstd = sem("s_rstd")
        s_xt = sem("s_xt")
        s_xt_ev = sem("s_xt_ev")
        s_qp = sem("s_qp")
        s_qp_ev = sem("s_qp_ev")
        s_ql = sem("s_ql")
        s_rope = sem("s_rope")
        s_rope_add = sem("s_rope_add")
        s_xt_low = sem("s_xt_low")
        s_hk_low = sem("s_hk_low")
        s_w_high = sem("s_w_high")
        s_w_low = {kind: sem(f"s_{kind}_low") for kind in ("wq", "wcq")}
        s_qd = sem("s_qd")
        s_qd_high = sem("s_qd_high")
        s_qd_low = sem("s_qd_low")
        s_krope = sem("s_krope")
        s_kt = sem("s_kt")
        s_kt_high = sem("s_kt_high")
        s_kt_low = sem("s_kt_low")
        s_score = sem("s_score")
        s_max = sem("s_max")
        s_exp = sem("s_exp")
        s_inv = sem("s_inv")
        s_norm = [sem(f"s_norm{i}") for i in range(2)]
        s_pt = sem("s_pt")
        s_pt_high = sem("s_pt_high")
        s_pt_low = sem("s_pt_low")
        s_ctx = sem("s_ctx")
        s_ctx_high = sem("s_ctx_high")
        s_ctx_low = sem("s_ctx_low")
        s_o = sem("s_o")
        s_x2 = sem("s_x2_made")
        s_route = sem("s_route")
        s_sh = sem("s_sh")
        s_sh_a = sem("s_sh_a")
        s_xn2_st = sem("s_xn2_st")
        s_base_st = sem("s_base_st")
        s_tab = [sem(f"s_tab{i}") for i in range(2)]

        def products(out_ap, weights, moving, first, last, signal):
            (wh, wl), (mh, ml) = weights, moving
            for n, (w, m) in enumerate(((wh, mh), (wh, ml), (wl, mh))):
                mark = pe.do(lambda e, w=w, m=m, n=n: e.matmul(out_ap, w, m, start=first and n == 0,
                                                               stop=last and n == 2), signal)
            return mark

        x_loaded = [None] * B
        x_used = [None] * B
        xt_ready = [None] * B
        xt_mm = [None] * B
        ln_ready = {}
        ln_used = [None] * (GB + 1)
        q_proj_over = None

        def layer_norm_stats(x_in, i):
            st, mv, rs = ln_stats[i][:, 0:6], ln_stats[i][:, 6:8], ln_stats[i][:, 0:1]
            dve.wait(ln_used[i])
            dve.wait(dve.do(lambda e: e.bn_stats(st, x_in), s_ln))
            pool.wait(dve.do(lambda e: e.bn_aggr(mv, st), s_ln))
            pool.wait(pool.do(lambda e: e.tensor_scalar(rs, mv[:, 1:2], EPS, None, ALU.add), s_rstd))
            return pool.do(lambda e: e.tensor_tensor(rs, rs, minus_half[0:S, :], ALU.pow), s_rstd)

        def layer_norm_apply(x_in, x_out, i, ready):
            mv, rs = ln_stats[i][:, 6:8], ln_stats[i][:, 0:1]
            dve.wait(ready)
            ln_used[i] = dve.do(lambda e: e.tensor_scalar(x_out, x_in, mv[:, 0:1], rs, ALU.subtract, ALU.mult), s_ln)
            return ln_used[i]

        def load_x(b):
            if b >= NX:
                sp.wait(x_used[b - NX])
            x_loaded[b] = sp.do(lambda e: e.dma_start(x_sb[b % NX][:], a["x"][b * S:(b + 1) * S, :]),
                                s_x[b % NX], 16)

        def stats_x(b):
            dve.wait(x_loaded[b])
            ln_ready[b] = layer_norm_stats(x_sb[b % NX][:], GB)

        def norm_x(b):
            dve.wait(xt_mm[b - 1] if b else None)
            ln_ready[b] = layer_norm_apply(x_sb[b % NX][:], xn1[:], GB, ln_ready[b])

        def turn_x(b):
            pe.wait(ln_ready[b], bank_read[7])
            for j in range(CJ):
                t = pe.do(lambda e, j=j: e.transpose(bank[7][:, j * S:(j + 1) * S], xn1[:, j * P:(j + 1) * P],
                                                     ident[0:S, 0:S]), s_xt)
            xt_mm[b] = t
            act.wait(t, q_proj_over)
            src = bank[7][:, 0:CJ * S].rearrange("p (j s) -> p j s", j=CJ)
            high, low = (x[:, :, b % GB, :] for x in xn_t)
            h = act.do(lambda e: e.activation(high, src, ACT.Copy), s_xt_ev)
            dve.wait(h)
            xt_ready[b] = bank_read[7] = dve.do(lambda e: e.tensor_tensor(low, src, high, ALU.subtract), s_xt_low)

        q_sin_free = {}
        kinds = ("wq", "wcq", "m_w")
        w_loaded = {kind: {} for kind in kinds}
        w_used = {kind: {} for kind in kinds}
        w_split = {kind: {} for kind in kinds}

        def load_weight(kind, n):
            if n >= NG * H:
                return
            h, i = n % H, n % NW
            dst, src = {"wq": (wq[i][:], a["w_q"][h]), "wcq": (wcq[i][:], a["w_cq"][h]),
                        "m_w": (m_w[i][:], m_dram[h].rearrange("p (c d) -> p c d", d=D))}[kind]
            sp.wait((w_used if kind == "m_w" else w_split)[kind].get(n - NW), m_stored[h] if kind == "m_w" else None)
            w_loaded[kind][n] = sp.do(lambda e: e.dma_start(dst, src), s_w[kind][i], 16)

        def split_weight(kind, n):
            if n >= NG * H:
                return
            full = {"wq": wq, "wcq": wcq}[kind][n % NW]
            high, low = {"wq": wq_s, "wcq": wcq_s}[kind][n % 2]
            act.wait(w_loaded[kind][n], w_used[kind].get(n - 2))
            h = act.do(lambda e: e.activation(high[:], full[:], ACT.Copy), s_w_high)
            queue = {"wq": pool, "wcq": dve}[kind]
            queue.wait(h)
            w_split[kind][n] = queue.do(lambda e: e.tensor_tensor(low[:], full[:], high[:], ALU.subtract), s_w_low[kind])
            load_weight(kind, n + NW)

        def query_phase(g, between):
            nonlocal q_proj_over
            hk_ready, rope_done, ql_done, qd_done, made = {}, {}, {}, {}, {}

            def project(h):
                n = g * H + h
                pe.wait(w_split["wq"][n], bank_read[0], *[xt_ready[g * GB + i] for i in range(GB)])
                for j in range(CJ):
                    m = products(bank[0][:, 0:GT], [w[:, j, :] for w in wq_s[n % 2]],
                                 [x[:, j, :, :].rearrange("p b s -> p (b s)") for x in xn_t], j == 0, j == CJ - 1, s_qp)
                w_used["wq"][n] = m
                high, low = q_hk[h % 2]
                act.wait(m, ql_done.get(h - 2))
                up = act.do(lambda e: e.activation(high[:], bank[0][:, 0:GT], ACT.Copy), s_qp_ev)
                dve.wait(up)
                hk_ready[h] = bank_read[0] = dve.do(lambda e: e.tensor_tensor(low[:], bank[0][:, 0:GT], high[:],
                                                                              ALU.subtract), s_hk_low)
                return m

            def latent(h):
                n = g * H + h
                pe.wait(w_split["wcq"][n], hk_ready[h])
                ready, order = {}, (0, 2, 1, 3)
                for c in order:
                    pe.wait(bank_read[1 + c])
                    ready[c] = m = (products(bank[1 + c][0:QW, 0:GT], [w[:, c * QW:(c + 1) * QW] for w in wcq_s[n % 2]],
                                          [x[:] for x in q_hk[h % 2]], True, True, s_ql))
                ql_done[h] = w_used["wcq"][n] = m
                for c in order:
                    dve.wait(ready[c], qd_done.get(h - 2), q_sin_free.get((c + QC // 2) % QC))
                    src = bank[1 + c][0:QW, 0:GT].rearrange("p (b s) -> p b s", b=GB)
                    for dst, tab, to in ((q_rope[h % 2], cos_q, c), (q_sin, sin_q, (c + QC // 2) % QC)):
                        r = dve.do(lambda e, d=dst, t=tab, to=to, src=src: e.tensor_tensor(
                            d[:, to, :].rearrange("p (b s) -> p b s", b=GB), src,
                            t[:, to, :].unsqueeze(1).to_broadcast([QW, GB, S]), ALU.mult), s_rope)
                    bank_read[1 + c] = made[c] = r
                for c in order:
                    pool.wait(made[c], made[(c + QC // 2) % QC])
                    q_sin_free[c] = pool.do(lambda e, c=c, o=q_rope[h % 2]: e.tensor_tensor(
                        o[:, c, :], o[:, c, :], q_sin[:, c, :], ALU.add), s_rope_add)
                    rope_done[h, c] = q_sin_free[c]

            def to_context(h):
                n = g * H + h
                pe.wait(w_loaded["m_w"][n], bank_read[5])
                for n_c, c in enumerate((0, 2, 1, 3)):
                    pe.wait(rope_done[h, c])
                    m = pe.do(lambda e, c=c, n_c=n_c: e.matmul(bank[5][:, 0:GT], m_w[n % NW][:, c, :], q_rope[h % 2][:, c, :],
                                                      start=(n_c == 0), stop=(n_c == QC - 1)), s_qd)
                qd_done[h] = w_used["m_w"][n] = m
                src = bank[5][:, 0:GT].rearrange("p (b s) -> p b s", b=GB)
                act.wait(m, *q_t_free)
                high = act.do(lambda e: e.activation(q_t[0][:, :, h, :], src, ACT.Copy), s_qd_high)
                dve.wait(high)
                mark = bank_read[5] = dve.do(lambda e: e.tensor_tensor(q_t[1][:, :, h, :], src, q_t[0][:, :, h, :],
                                                                       ALU.subtract), s_qd_low)
                return mark

            for h in range(H + 2):
                if h < H:
                    split_weight("wq", g * H + h + 1)
                    split_weight("wcq", g * H + h)
                    last = project(h)
                if 1 <= h <= H:
                    latent(h - 1)
                if h >= 2:
                    q_ready = to_context(h - 2)
                if h >= 2:
                    load_weight("m_w", g * H + h - 2 + NW)
                for fn in between.get(h, ()):
                    fn()
            q_proj_over = last
            return q_ready

        q_t_free = []
        kv_ready = [None] * B
        kvr_ready = [None] * B
        kv_used = [None] * B
        krope_free = [None]
        scores_over = [None] * B

        def rope_context(b):
            i = b % 2
            sp.wait(krope_free[0])
            loaded = sp.do(lambda e: e.dma_start(kv_raw[:], a["ctx"][b].rearrange("(j p) d -> p j d", p=LP)), s_kv, 16)
            dve.wait(loaded, const_loaded, kv_turned[0])
            hd = D // 2
            dve.do(lambda e: e.tensor_tensor(kv_full[:], kv_raw[:], cos_k[:], ALU.mult), s_krope)
            dve.do(lambda e: e.tensor_tensor(kv_tmp[:, :, 0:hd], kv_raw[:, :, hd:D], sin_k[:, :, 0:hd], ALU.mult), s_krope)
            m = dve.do(lambda e: e.tensor_tensor(kv_tmp[:, :, hd:D], kv_raw[:, :, 0:hd], sin_k[:, :, hd:D], ALU.mult),
                        s_krope)
            krope_free[0] = m
            dve.wait(m)
            f = dve.do(lambda e: e.tensor_tensor(kv_full[:], kv_full[:], kv_tmp[:], ALU.add), s_krope)
            dve.wait(f, kv_used[b - 2] if b >= 2 else None)
            high, low = kv_r[i]
            dve.wait(dve.do(lambda e: e.tensor_copy(high[:], kv_full[:]), s_krope))
            kvr_ready[b] = dve.do(lambda e: e.tensor_tensor(low[:], kv_full[:], high[:], ALU.subtract), s_krope)

        kv_turned = [None]

        def turn_context(b):
            pe.wait(kvr_ready[b], bank_read[7])
            for j in range(LJ):
                t = pe.do(lambda e, j=j: e.transpose(bank[7][:, j * LP:(j + 1) * LP], kv_full[:, j, :],
                                                     ident[0:LP, 0:LP]), s_kt)
            kv_turned[0] = t
            high, low = kv_t[b % 2]
            act.wait(t, scores_over[b - 2] if b >= 2 else None)
            h = act.do(lambda e: e.activation(high[:, 0:L], bank[7][:, 0:L], ACT.Copy), s_kt_high)
            dve.wait(h)
            kv_ready[b] = bank_read[7] = dve.do(lambda e: e.tensor_tensor(low[:, 0:L], bank[7][:, 0:L], high[:, 0:L],
                                                                          ALU.subtract), s_kt_low)

        tile_norm, pt_read, exp_done, pt_mm = {}, {}, {}, {}
        ctx_mm = {}
        ctx_ev = {}
        NBK = -(-RT // TB)

        def score_tile(b, t, q_ready):
            n = b * RT + t
            bk, i = n % 3, n % NP
            pe.wait(q_ready, kv_ready[b], bank_read[bk])
            rows = [q[:, b % GB, :, :].rearrange("d h s -> d (h s)")[:, t * P:(t + 1) * P] for q in q_t]
            m = scores_over[b] = products(bank[bk][:, 0:L + 1], rows, [k[:] for k in kv_t[b % 2]], True, True, s_score)
            dve.wait(m, exp_done.get(n - NP))
            mx = dve.do(lambda e: e.tensor_reduce(row_max[:, i:i + 1], bank[bk][:, 0:L], AX_X, ALU.max, negate=True), s_max)
            max_done[n] = mx

        def exponentials(b, t):
            n = b * RT + t
            bk, i = n % 3, n % NP
            act.wait(max_done[n], pt_mm.get(n - NP), inv_done.get(n - NP))
            exp_done[n] = bank_read[bk] = act.do(
                lambda e: e.activation(prob[i][:], bank[bk][:, 0:L], ACT.Exp, bias=row_max[:, i:i + 1],
                                       accum_out=row_sum[:, i:i + 1]), s_exp)

        inv_done, max_done = {}, {}

        def reciprocals(b, t):
            n = b * RT + t
            i = n % NP
            dve.wait(exp_done[n], tile_norm.get(n - NP))
            inv_done[n] = dve.do(lambda e: e.reciprocal(row_inv[:, i:i + 1], row_sum[:, i:i + 1]), s_inv)

        def normalise(b, t):
            n = b * RT + t
            i = n % NP
            if n % 2:
                pool.wait(inv_done[n])
                tile_norm[n] = pool.do(lambda e: e.tensor_scalar(prob[i][:], prob[i][:], row_inv[:, i:i + 1], None,
                                                                 ALU.mult), s_norm[1])
            else:
                act.wait(inv_done[n])
                tile_norm[n] = act.do(lambda e: e.activation(prob[i][:], prob[i][:], ACT.Copy, scale=row_inv[:, i:i + 1]),
                                      s_norm[0])

        def turn_tile(b, t):
            n = b * RT + t
            i, bk = n % NP, 3 + n % 2
            blk = b * NBK + t // TB
            pe.wait(tile_norm[n], bank_read[bk])
            for j in range(LJ):
                m = pe.do(lambda e, j=j: e.transpose(bank[bk][0:LP, j * P:(j + 1) * P], prob[i][:, j * LP:(j + 1) * LP],
                                                     ident[:]), s_pt)
            pt_mm[n] = m

        def split_tile_high(b, t):
            n = b * RT + t
            bk = 3 + n % 2
            blk = b * NBK + t // TB
            src = bank[bk][0:LP, 0:LJ * P].rearrange("p (j r) -> p j r", j=LJ)
            high, low = (p[:, :, (t % TB) * P:(t % TB + 1) * P] for p in prob_t[blk % 2])
            act.wait(pt_mm[n], ctx_mm.get(blk - 2))
            h = act.do(lambda e: e.activation(high, src, ACT.Copy), s_pt_high)

            def split_low():
                dve.wait(h)
                split_tile_low(n, bk, low, src, high)
            return split_low

        def split_tile_low(n, bk, low, src, high):
            pt_read[n] = bank_read[bk] = dve.do(lambda e: e.tensor_tensor(low, src, high, ALU.subtract), s_pt_low)

        def attend(b, blk):
            n, width = b * NBK + blk, min(TB, RT - TB * blk) * P
            bk = 5 + n % 2
            pe.wait(pt_read[b * RT + min(TB * blk + TB - 1, RT - 1)], kvr_ready[b], bank_read[bk])
            for j in range(LJ):
                m = products(bank[bk][:, 0:width], [k[:, j, :] for k in kv_r[b % 2]],
                             [p[:, j, 0:width] for p in prob_t[n % 2]], j == 0, j == LJ - 1, s_ctx)
            ctx_mm[n] = kv_used[b] = m
            return lambda: attended(b, blk, n, width, bk, m)

        def attended(b, blk, n, width, bk, m):
            high, low = (q[:, b % GB, :, :].rearrange("d h s -> d (h s)")[:, blk * TB * P:blk * TB * P + width] for q in q_t)
            act.wait(m)
            h = act.do(lambda e: e.activation(high, bank[bk][:, 0:width], ACT.Copy), s_ctx_high)
            dve.wait(h)
            ctx_ev[b] = bank_read[bk] = dve.do(lambda e: e.tensor_tensor(low, bank[bk][:, 0:width], high, ALU.subtract),
                                               s_ctx_low)

        v_loaded, v_split, v_used = [], [], []

        def load_v(n):
            h, i = n % H, n % NV
            sp.wait(v_split[n - NV] if n >= NV else None, v_stored[h])
            v_loaded.append(sp.do(lambda e: e.dma_start(v_raw[i][:], v_dram[h]), s_vl[i], 16))

        def split_v(n):
            i = n % NV
            act.wait(v_loaded[n], v_used[n - NV] if n >= NV else None)
            high = act.do(lambda e: e.activation(v_w[i][0][:], v_raw[i][:], ACT.Copy), s_v_high)
            dve.wait(high)
            v_split.append(dve.do(lambda e: e.tensor_tensor(v_w[i][1][:], v_raw[i][:], v_w[i][0][:], ALU.subtract), s_v_low))
            if n + NV < NG * H:
                load_v(n + NV)

        def project_out(g):
            batches = range(g * GB, (g + 1) * GB)
            pe.wait(*[ctx_ev[b] for b in batches], *[bank_read[4 + i] for i in range(GB)])
            for h in range(H):
                n = g * H + h
                if h == 0:
                    split_v(n)
                if h + 1 < H:
                    split_v(n + 1)
                pe.wait(v_split[n])
                for i in range(GB):
                    m = products(bank[4 + i][0:S, :], [q[:, i, h, :] for q in q_t],
                                 [v[:] for v in v_w[n % NV]], h == 0, h == H - 1, s_o)
                v_used.append(m)
            q_t_free[:] = [m]
            for b in batches:
                x = x_sb[b % NX]
                dve.wait(m, tanh_done)
                r = bank_read[4 + b % GB] = dve.do(lambda e, b=b, x=x: e.scalar_tensor_tensor(
                    x[:], bank[4 + b % GB][0:S, :], tanh_g[0:S, 0:1], x[:], ALU.mult, ALU.add), s_x2)
                dve.wait(r)
                ln_ready[B + b] = layer_norm_stats(x[:], b % GB)

        base_done, xn2_turned, xn2_ready, xn2t_ready, sh_ready = [None], [None], [None], [None], [None]
        xn2t_used = [None]
        route_done = [None]
        xn2_stored, base_stored = [None], [None]
        scattered = [None, None]
        mask_used, rank_used = [None], [None]

        def norm_x2(b):
            dve.wait(xn2_stored[0], xn2_turned[0])
            xn2_ready[0] = n = layer_norm_apply(x_sb[b % NX][:], xn2[:], b % GB, ln_ready[B + b])
            sp.wait(n)
            xn2_stored[0] = sp.do(lambda e: e.dma_start(xn2_dram[b * S:(b + 1) * S, :], xn2[:]), s_xn2_st, 16)

        def turn_xn2(b):
            pe.wait(xn2_ready[0], bank_read[7])
            for j in range(CJ):
                m = pe.do(lambda e, j=j: e.transpose(bank[7][:, j * S:(j + 1) * S], xn2[:, j * P:(j + 1) * P],
                                                     ident[0:S, 0:S]), s_xt)
            xn2_turned[0] = m
            act.wait(m, xn2t_used[0])
            xn2t_ready[0] = bank_read[7] = act.do(
                lambda e: e.activation(xn2_t[:], bank[7][:, 0:CJ * S].rearrange("p (j s) -> p j s", j=CJ), ACT.Copy),
                s_xt_ev)

        def router_and_shared_in(b):
            pe.wait(xn2t_ready[0], bank_read[6])
            parts = [(bank[6][0:S, 0:E + 1], lambda j: xn2_t[:, j, :], lambda j: router_w[:, j, :]),
                     (bank[6][:, 128:128 + S], lambda j: shared_in[:, j, 0:I], lambda j: xn2_t[:, j, :]),
                     (bank[6][:, 256:256 + S], lambda j: shared_in[:, j, I:2 * I], lambda j: xn2_t[:, j, :])]
            for o, lhs, rhs in parts:
                for j in range(CJ):
                    m = pe.do(lambda e, o=o, w=lhs(j), x=rhs(j), j=j: e.matmul(o, w, x, start=(j == 0), stop=(j == CJ - 1)),
                              s_sh)
            xn2t_used[0] = m
            gate, up = bank[6][:, 128:128 + S], bank[6][:, 256:256 + S]
            act.wait(m, base_done[0])
            act.do(lambda e: e.activation(sh_t[:], gate, ACT.Tanh, scale=0.5), s_sh_a)
            th = act.do(lambda e: e.activation(small[:, 0:1], bank[6][0:S, E:E + 1], ACT.Tanh, scale=0.5), s_sh_a)
            dve.wait(th, route_done[0])
            dve.do(lambda e: e.tensor_copy(logit[:], bank[6][0:S, 0:E + 1]), s_route)
            v = dve.do(lambda e: e.scalar_tensor_tensor(sh_v[:], sh_t[:], 1.0, gate, ALU.add, ALU.mult), s_route)
            dve.wait(v)
            sh_ready[0] = bank_read[6] = dve.do(
                lambda e: e.scalar_tensor_tensor(sh_w[:], sh_v[:], 0.5, up, ALU.mult, ALU.mult), s_route)

        def shared_down(b):
            pe.wait(sh_ready[0], bank_read[6])
            m = pe.do(lambda e: e.matmul(bank[6][0:S, :], sh_w[:], shared_out[:], start=True, stop=True), s_sh)
            dve.wait(m)
            dve.wait(dve.do(lambda e: e.tensor_scalar(small[:, 1:2], small[:, 0:1], 1.0, 0.5, ALU.add, ALU.mult), s_route))
            dve.wait(dve.do(lambda e: e.tensor_tensor(small[:, 2:3], small[:, 1:2], tanh_g[0:S, 1:2], ALU.mult), s_route))
            base_done[0] = bank_read[6] = dve.do(lambda e: e.scalar_tensor_tensor(
                x_sb[b % NX][:], bank[6][0:S, :], small[:, 2:3], x_sb[b % NX][:], ALU.mult, ALU.add), s_route)
            sp.wait(base_done[0])
            x_used[b] = base_stored[0] = sp.do(
                lambda e: e.dma_start(out[b * S:(b + 1) * S, :], x_sb[b % NX][:]), s_base_st, 16)

        def chain(fn):
            mark = dve.do(fn, s_route)
            dve.wait(mark)
            return mark

        def choose(b):
            lg = logit[:, 0:E]
            dve.wait((s_route, counts[id(s_route)]))
            if b == 0:
                dve.do(lambda e: e.memset(count[:], 0.0), s_route)
            chain(lambda e: e.max(top[:], lg))
            dve.do(lambda e: e.max_index(top_i[:], top[:], lg), s_route)
            chain(lambda e: e.match_replace(out=left[:], in_to_replace=top[:], in_values=lg, imm_value=-3.4028235e38))
            if mask_used[0] is not None:
                dve.wait(mask_used[0])
            mk = chain(lambda e: e.tensor_tensor(mask[:], left[:], lg, ALU.not_equal))
            dve.do(lambda e: e.tensor_copy(pair[:, 0, :], top_i[:]), s_route)
            mx = chain(lambda e: e.tensor_scalar(small[:, 3:4], top[:, 0:1], -1.0, None, ALU.mult))
            act.wait(mx)
            ex = act.do(lambda e: e.activation(pair[:, 1, :], top[:], ACT.Exp, bias=small[:, 3:4],
                                               accum_out=small[:, 4:5]), s_sh_a)
            pe.wait(mk, bank_read[7])
            pe.do(lambda e: e.matmul(bank[7][0:S, 0:E], before[:], mask[:], start=True, stop=False), s_sh)
            rank = pe.do(lambda e: e.matmul(bank[7][0:S, 0:E], ones[:, 0:S], count[:], start=False, stop=True), s_sh)
            dve.wait(ex)
            chain(lambda e: e.reciprocal(small[:, 5:6], small[:, 4:5]))
            chain(lambda e: e.tensor_tensor(small[:, 6:7], small[:, 5:6], tanh_g[0:S, 1:2], ALU.mult))
            dve.do(lambda e: e.tensor_scalar(weight[b % 2][:], pair[:, 1, :], small[:, 6:7], None, ALU.mult), s_route)
            act.wait(rank, rank_used[0])
            bank_read[7] = act.do(lambda e: e.activation(rank_sb[:], bank[7][0:S, 0:E], ACT.Copy), s_sh_a)
            return bank_read[7]

        mask_used, rank_used = [None], [None]

        def place(b, rank):
            dve.wait(rank)
            for k in range(TOP):
                if k:
                    dve.wait(last)
                last = dve.do(lambda e, k=k: e.scalar_tensor_tensor(
                    scratch_e[:], expert[:], pair[:, 0, k:k + 1], rank_sb[:], ALU.is_equal, ALU.mult,
                    accum_out=pair[:, 2, k:k + 1]), s_route)
            rank_used[0] = last
            dve.wait(last)
            mask_used[0] = dve.do(lambda e: e.tensor_tensor(count[:], count[:], mask[:], ALU.add), s_route)
            ex, r, m, q, t, f, g1 = (pair[:, n, :] for n in (0, 2, 3, 4, 5, 6, 7))
            chain(lambda e: e.tensor_scalar(q, r, -(TR - 1) / 2, 1.0 / TR, ALU.add, ALU.mult))
            chain(lambda e: e.tensor_scalar(q, q, ROUND, -ROUND, ALU.add, ALU.add))
            chain(lambda e: e.scalar_tensor_tensor(m, q, -float(TR), r, ALU.mult, ALU.add))
            chain(lambda e: e.tensor_scalar(f, q, float(MT), None, ALU.is_lt))
            chain(lambda e: e.tensor_scalar(t, q, float(E), None, ALU.mult))
            chain(lambda e: e.tensor_tensor(t, t, ex, ALU.add))
            chain(lambda e: e.tensor_scalar(q, q, float(1 - E), None, ALU.mult))
            chain(lambda e: e.scalar_tensor_tensor(g1, ex, float(MT - 1), q, ALU.mult, ALU.add))
            chain(lambda e: e.tensor_tensor(g1, g1, f, ALU.mult))
            chain(lambda e: e.tensor_tensor(t, t, g1, ALU.add))
            dve.wait(scattered[b % 2])
            dve.do(lambda e: e.tensor_copy(entry[b % 2][:, :, 0], token[:, b:b + 1].to_broadcast([S, TOP])), s_route)
            chain(lambda e: e.tensor_copy(entry[b % 2][:, :, 1].bitcast(F32), weight[b % 2][:]))
            ready = route_done[0] = dve.do(lambda e: e.scalar_tensor_tensor(
                pos_i[b % 2][:], m, float(NT), t, ALU.mult, ALU.add), s_route)
            dve.wait(ready)

        def scatter(b, ks):
            pool.wait(route_done[0], table_clear)
            for k in ks:
                scattered[b % 2] = pool.do(lambda e, k=k: e.indirect_dma_start(
                    table, bass.IndirectOffsetOnAxis(ap=pos_i[b % 2][:, k:k + 1], axis=0), entry[b % 2][:, k, :], None),
                    s_tab[b % 2], 16)

        pe.wait(const_loaded)
        for b in range(GB):
            load_x(b)
        q_t_free[:] = fold_weights()
        for n in range(NW):
            for kind in kinds:
                load_weight(kind, n)
        split_weight("wq", 0)
        for b in range(GB):
            stats_x(b)
            norm_x(b)
            turn_x(b)
        rope_context(0)
        turn_context(0)
        for n in range(NV):
            load_v(n)
        LAG = 4

        def finish_batch(b, stage):
            if stage == 0:
                norm_x2(b)
            if stage == 1:
                turn_xn2(b)
            if stage == 2:
                router_and_shared_in(b)
            if stage == 3:
                shared_down(b)
                ranks[b] = choose(b)
            if stage == 4:
                place(b, ranks[b])
                scatter(b, range(TOP // 2))
            if stage == 5:
                scatter(b, range(TOP // 2, TOP))

        ranks = {}
        between = {}
        for g in range(NG):
            q_ready = query_phase(g, between)
            tiles = [(b, i) for b in range(g * GB, (g + 1) * GB) for i in range(RT)]
            attend_due, evacuate_due = {}, []
            for t in range(len(tiles) + LAG + 4):
                if 0 <= t - 2 < len(tiles):
                    reciprocals(*tiles[t - 2])
                if t < len(tiles):
                    score_tile(*tiles[t], q_ready)
                if 0 <= t - LAG < len(tiles):
                    turn_tile(*tiles[t - LAG])
                for evacuate in evacuate_due:
                    evacuate()
                evacuate_due = []
                for b, blk in attend_due.pop(t, ()):
                    evacuate_due.append(attend(b, blk))
                low = split_tile_high(*tiles[t - LAG]) if 0 <= t - LAG < len(tiles) else None
                if 0 <= t - 1 < len(tiles):
                    exponentials(*tiles[t - 1])
                if 0 <= t - 2 < len(tiles):
                    normalise(*tiles[t - 2])
                if low:
                    low()
                    b, i = tiles[t - LAG]
                    if i % TB == TB - 1 or i == RT - 1:
                        attend_due.setdefault(t + 2, []).append((b, i // TB))
                if t < len(tiles):
                    b, i = tiles[t]
                    if b + 1 < B:
                        if i == 8:
                            rope_context(b + 1)
                        if i == 11:
                            turn_context(b + 1)
                    if b + GB < B:
                        if i == 0:
                            load_x(b + GB)
                        if i == 2:
                            stats_x(b + GB)
                        if i == 5:
                            norm_x(b + GB)
                        if i == 7:
                            turn_x(b + GB)
            project_out(g)
            between = {}
            for i in range(GB):
                for stage in range(6):
                    between.setdefault(4 * i + stage, []).append(
                        lambda b=g * GB + i, stage=stage: finish_batch(b, stage))
        for step in sorted(between):
            for fn in between[step]:
                fn()
        attention_over = [route_done[0], mask_used[0], *scattered, base_stored[0], xn2_stored[0]]
        att_ctx.close()
        sb = kept_sb

        NE = 3
        w_gu = [sb(f"w_gu{i}", [P, CJ, 2 * I]) for i in range(NE)]
        w_dp = [sb(f"w_dp{i}", [I, C]) for i in range(NE)]
        w_gu_s = [[sb(f"w_gu_s{i}{p}", [P, CJ, 2 * I], F32R) for p in "hl"] for i in range(2)]
        w_dp_s = [[sb(f"w_dp_s{i}{p}", [I, C], F32R) for p in "hl"] for i in range(3)]
        index = sb("index", [TR, MT * E, 2], I32)
        NXG = 3 * MT
        x_g = [sb(f"x_g{i}", [TR, C]) for i in range(NXG)]
        xg_t = [[sb(f"xg_t{i}{p}", [P, CJ, CAP], F32R) for p in "hl"] for i in range(2)]
        e_tanh = [sb(f"e_tanh{i}", [I, CAP]) for i in range(2)]
        e_half = [sb(f"e_half{i}", [I, CAP]) for i in range(2)]
        e_inner = [sb(f"e_inner{i}", [I, CAP]) for i in range(2)]
        e_inner_s = [[sb(f"e_inner_s{i}{p}", [I, CAP], F32R) for p in "hl"] for i in range(2)]
        NY = 2 * MT
        y_sb = [sb(f"y_sb{i}", [TR, C]) for i in range(NY)]
        total = sb("total", [S, 4])

        s_ew = [sem(f"s_ew{i}") for i in range(NE)]
        s_ws_a = sem("s_ws_a")
        s_ws_v = sem("s_ws_v")
        s_index = sem("s_index")
        s_xg = [sem(f"s_xg{i}") for i in range(NXG)]
        s_et = sem("s_et")
        s_et_a = sem("s_et_a")
        s_et_v = sem("s_et_v")
        s_gu = sem("s_gu")
        s_tanh_e = sem("s_tanh_e")
        s_inner = sem("s_inner")
        s_down = sem("s_down")
        s_y_a = sem("s_y_a")
        s_y_v = sem("s_y_v")
        s_add = [sem(f"s_add{i}") for i in range(NY)]
        s_rounds = sem("s_rounds")

        for queue in (pe, dve, act, pool, sp):
            queue.wait(*attention_over)

        totals = pe.do(lambda e: e.matmul(bank[7][0:S, 0:E], ones[:, 0:S], count[:], start=True, stop=True), s_et)
        dve.wait(totals)
        for fn in (lambda e: e.tensor_reduce(total[:, 0:1], bank[7][0:S, 0:E], AX_X, ALU.max),
                   lambda e: e.tensor_scalar(total[:, 1:2], total[:, 0:1], (TR - 1) / 2 - CAP, 1.0 / TR, ALU.add, ALU.mult),
                   lambda e: e.tensor_scalar(total[:, 2:3], total[:, 1:2], ROUND, -ROUND, ALU.add, ALU.add),
                   lambda e: e.tensor_scalar(total[:, 3:4], total[:, 2:3], 0.0, float(ROUNDS), ALU.max, ALU.min),
                   lambda e: e.tensor_copy(rounds[:], total[0:1, 3:4])):
            rounds_ready = dve.do(fn, s_rounds)
            dve.wait(rounds_ready)
        bank_read[7] = rounds_ready

        index_loaded = sp.do(lambda e: e.dma_start(index[:], table_3d[:, 0:MT * E, :]), s_index, 16)
        ew_loaded, ew_split, down_done, gathered, turned, gu_done, inner_done = {}, {}, {}, {}, {}, {}, {}
        xt_high, xt_low, y_ready, added = {}, {}, {}, {}

        def load_expert(x):
            sp.wait(ew_split.get(x - NE))
            for dst, src in ((w_gu[x % NE][:], a["w_gu"][x]), (w_dp[x % NE][:], a["w_dp"][x])):
                ew_loaded[x] = sp.do(lambda e, d=dst, s=src: e.dma_start(d, s), s_ew[x % NE], 16)

        def split_expert(x):
            for full, (high, low), used in ((w_gu[x % NE], w_gu_s[x % 2], gu_done.get(x - 2)),
                                            (w_dp[x % NE], w_dp_s[x % 3], down_done.get(x - 3))):
                act.wait(ew_loaded[x], used)
                h = act.do(lambda e, o=high, i=full: e.activation(o[:], i[:], ACT.Copy), s_ws_a)
                dve.wait(h)
                ew_split[x] = dve.do(lambda e, o=low, i=full, h=high: e.tensor_tensor(o[:], i[:], h[:], ALU.subtract), s_ws_v)

        def gather(x):
            pool.wait(index_loaded, turned.get(x - NXG // MT))
            for i in range(MT):
                n = x * MT + i
                gathered[n] = pool.do(lambda e, n=n: e.indirect_dma_start(
                    x_g[n % NXG][:], None, xn2_dram, bass.IndirectOffsetOnAxis(ap=index[:, n, 0:1], axis=0)),
                    s_xg[n % NXG], 16)

        def turn(x):
            high, low = xg_t[x % 2]
            for i in range(MT):
                n = x * MT + i
                bk = n % 3
                pe.wait(gathered[n], bank_read[bk])
                for j in range(CJ):
                    m = pe.do(lambda e, n=n, j=j, bk=bk: e.transpose(
                        bank[bk][:, j * TR:(j + 1) * TR], x_g[n % NXG][:, j * P:(j + 1) * P], ident[0:TR, 0:TR]), s_et)
                turned[x] = m
                src = bank[bk][:, 0:CJ * TR].rearrange("p (j t) -> p j t", j=CJ)
                act.wait(m, gu_done.get(x - 2))
                h = act.do(lambda e, i=i, src=src: e.activation(high[:, :, i * TR:(i + 1) * TR], src, ACT.Copy), s_et_a)
                dve.wait(h)
                xt_low[x] = bank_read[bk] = dve.do(lambda e, i=i, src=src: e.tensor_tensor(
                    low[:, :, i * TR:(i + 1) * TR], src, high[:, :, i * TR:(i + 1) * TR], ALU.subtract), s_et_v)

        def inner(x):
            g, u = 3, 4
            pe.wait(ew_split[x], xt_low[x], bank_read[g], bank_read[u])
            for bk, at in ((g, 0), (u, I)):
                for j in range(CJ):
                    m = products(bank[bk][:, 0:CAP], [w[:, j, at:at + I] for w in w_gu_s[x % 2]],
                                 [t[:, j, :] for t in xg_t[x % 2]], j == 0, j == CJ - 1, s_gu)
            gu_done[x] = m
            i = x % 2
            high, low = e_inner_s[i]
            act.wait(m, inner_done.get(x - 2))
            t = act.do(lambda e: e.activation(e_tanh[i][:], bank[g][:, 0:CAP], ACT.Tanh, scale=0.5), s_tanh_e)
            dve.wait(t, down_done.get(x - 2))
            v = dve.do(lambda e: e.scalar_tensor_tensor(e_half[i][:], e_tanh[i][:], 1.0, bank[g][:, 0:CAP], ALU.add,
                                                        ALU.mult), s_inner)
            dve.wait(v)
            w = bank_read[g] = bank_read[u] = dve.do(lambda e: e.scalar_tensor_tensor(
                e_inner[i][:], e_half[i][:], 0.5, bank[u][:, 0:CAP], ALU.mult, ALU.mult), s_inner)
            dve.wait(w)
            dve.wait(dve.do(lambda e: e.tensor_copy(high[:], e_inner[i][:]), s_inner))
            inner_done[x] = dve.do(lambda e: e.tensor_tensor(low[:], e_inner[i][:], high[:], ALU.subtract), s_inner)

        def down(x):
            for i in range(MT):
                n = x * MT + i
                bk = 5 + n % 3
                pe.wait(inner_done[x], bank_read[bk])
                m = products(bank[bk][0:TR, :], [w[:, i * TR:(i + 1) * TR] for w in e_inner_s[x % 2]],
                             [w[:] for w in w_dp_s[x % 3]], True, True, s_down)
                down_done[x] = m
                w = index[:, n, 1:2].bitcast(F32)
                if i % 2:
                    dve.wait(m, added.get(n - NY), index_loaded)
                    r = dve.do(lambda e, n=n, bk=bk, w=w: e.tensor_scalar(y_sb[n % NY][:], bank[bk][0:TR, :], w, None,
                                                                          ALU.mult), s_y_v)
                else:
                    act.wait(m, added.get(n - NY), index_loaded)
                    r = act.do(lambda e, n=n, bk=bk, w=w: e.activation(y_sb[n % NY][:], bank[bk][0:TR, :], ACT.Copy,
                                                                       scale=w), s_y_a)
                bank_read[bk] = y_ready[n] = r

        def add(x):
            if x:
                pool.wait(*[added[n] for n in range((x - 1) * MT, x * MT)])
            for n in range(x * MT, (x + 1) * MT):
                pool.wait(y_ready[n])
                added[n] = pool.do(lambda e, n=n: e.indirect_dma_start(
                    out, bass.IndirectOffsetOnAxis(ap=index[:, n, 0:1], axis=0), y_sb[n % NY][:], None,
                    compute_op=ALU.add), s_add[n % NY], 16)

        for x in range(3):
            load_expert(x)
            gather(x)
        turn(0)
        split_expert(0)
        for x in range(E + 1):
            if x + 3 < E:
                load_expert(x + 3)
                gather(x + 3)
            if x + 1 < E:
                turn(x + 1)
                split_expert(x + 1)
            if x < E:
                inner(x)
            if x >= 1:
                down(x - 1)
                add(x - 1)
        adds_over = [added[n] for n in range((E - 1) * MT, E * MT)]

        lp = {n: sem(f"s_loop_{n}") for n in ("load", "gather", "turn", "turned", "gu", "tanh", "half", "inner", "down",
                                              "y", "stored")}
        s_loop_gather = sem("s_loop_gather_dma")
        s_loop_add = sem("s_loop_add_dma")
        l_index = sb("l_index", [TR, 2], I32)
        l_xt = sb("l_xt", [P, CJ, TR])

        def take(eng, name, value=1):
            eng.wait_ge(lp[name], value)
            eng.sem_clear(lp[name])

        def loop(body):
            def run(eng):
                n = eng.value_load(rounds[0:1, 0:1], min_val=0, max_val=ROUNDS)
                with eng.If(n > 0):
                    with eng.Fori(0, n) as r:
                        with eng.Fori(0, E) as x:
                            body(eng, r, x)
            return run

        def loop_sp(eng, r, x):
            tile = (r + MT) * E + x
            eng.dma_start(w_gu[0][:], a["w_gu"][bass.ds(x, 1)].rearrange("one p j i -> p (one j) i"))\
               .then_inc(lp["load"], 16)
            eng.dma_start(w_dp[0][:], a["w_dp"][bass.ds(x, 1)].rearrange("one i c -> i (one c)")).then_inc(lp["load"], 16)
            eng.dma_start(l_index[:], table_3d[:, bass.ds(tile, 1), :].rearrange("r one w -> r (one w)"))\
               .then_inc(lp["load"], 16)
            take(eng, "stored")

        def loop_pool(eng, r, x):
            take(eng, "load", 48)
            eng.indirect_dma_start(x_g[0][:], None, xn2_dram, bass.IndirectOffsetOnAxis(ap=l_index[:, 0:1], axis=0))\
               .then_inc(s_loop_gather, 16)
            eng.wait_ge(s_loop_gather, (r * E + x + 1) * 16)
            eng.nop().then_inc(lp["gather"], 1)
            take(eng, "y")
            eng.indirect_dma_start(out, bass.IndirectOffsetOnAxis(ap=l_index[:, 0:1], axis=0), y_sb[0][:], None,
                                   compute_op=ALU.add).then_inc(s_loop_add, 16)
            eng.wait_ge(s_loop_add, (r * E + x + 1) * 16)
            eng.nop().then_inc(lp["stored"], 1)

        def loop_pe(eng, r, x):
            take(eng, "gather")
            for j in range(CJ):
                m = eng.transpose(bank[0][:, j * TR:(j + 1) * TR], x_g[0][:, j * P:(j + 1) * P], ident[0:TR, 0:TR])
            m.then_inc(lp["turn"], 1)
            take(eng, "turned")
            for bk, at in ((2, 0), (3, I)):
                for j in range(CJ):
                    m = eng.matmul(bank[bk][:, 0:TR], w_gu[0][:, j, at:at + I], l_xt[:, j, :],
                                   start=(j == 0), stop=(j == CJ - 1))
            m.then_inc(lp["gu"], 1)
            take(eng, "inner")
            eng.matmul(bank[6][0:TR, :], e_inner[0][:, 0:TR], w_dp[0][:], start=True, stop=True).then_inc(lp["down"], 1)

        def loop_act(eng, r, x):
            take(eng, "turn")
            eng.activation(l_xt[:], bank[0][:, 0:CJ * TR].rearrange("p (j t) -> p j t", j=CJ), ACT.Copy)\
               .then_inc(lp["turned"], 1)
            take(eng, "gu")
            eng.activation(e_tanh[0][:, 0:TR], bank[2][:, 0:TR], ACT.Tanh, scale=0.5).then_inc(lp["tanh"], 1)
            take(eng, "down")
            eng.activation(y_sb[0][:], bank[6][0:TR, :], ACT.Copy, scale=l_index[:, 1:2].bitcast(F32))\
               .then_inc(lp["y"], 1)

        def loop_dve(eng, r, x):
            take(eng, "tanh")
            eng.scalar_tensor_tensor(e_half[0][:, 0:TR], e_tanh[0][:, 0:TR], 1.0, bank[2][:, 0:TR], ALU.add,
                                     ALU.mult).then_inc(lp["half"], 1)
            take(eng, "half")
            eng.scalar_tensor_tensor(e_inner[0][:, 0:TR], e_half[0][:, 0:TR], 0.5, bank[3][:, 0:TR], ALU.mult,
                                     ALU.mult).then_inc(lp["inner"], 1)

        for queue, body in ((sp, loop_sp), (pool, loop_pool), (pe, loop_pe), (act, loop_act), (dve, loop_dve)):
            queue.wait(rounds_ready, *adds_over)
            queue.ops.append(loop(body))

        block = ctx.enter_context(nc.Block())
        block.sync(sp.play)
        block.tensor(pe.play)
        block.vector(dve.play)
        block.scalar(act.play)
        block.gpsimd(pool.play)


def lay_out(x, ctx_512, g_xattn, g_ffn, L0_xattn_Wq, L0_xattn_w_kc_q, L0_xattn_w_kc_kv, L0_xattn_W_qr, L0_xattn_W_kr,
            L0_xattn_Wo, L0_ffn_gate_w, L0_ffn_gu_w, L0_ffn_dp_w, L0_ffn_sh_gate_w, L0_ffn_sh_up_w, L0_ffn_sh_down_w,
            L0_ffn_sh_gate1_w):
    cut = lambda w: np.asarray(w).T.reshape(CJ, P, -1).transpose(1, 0, 2)
    arrays = {
        "x": np.asarray(x).reshape(B * S, C),
        "ctx": np.asarray(ctx_512),
        "g_xattn": np.asarray(g_xattn), "g_ffn": np.asarray(g_ffn),
        "w_q": np.asarray(L0_xattn_Wq).reshape(H, K, CJ, P).transpose(0, 3, 2, 1),
        "w_cq": np.asarray(L0_xattn_w_kc_q),
        "w_qr": np.asarray(L0_xattn_W_qr).transpose(2, 0, 1),
        "w_kr": np.asarray(L0_xattn_W_kr).transpose(2, 0, 1),
        "w_kv": np.asarray(L0_xattn_w_kc_kv).transpose(1, 0, 2),
        "w_o": np.asarray(L0_xattn_Wo).reshape(C, H, K).transpose(1, 2, 0),
        "router_w": cut(np.concatenate([np.asarray(L0_ffn_gate_w), np.asarray(L0_ffn_sh_gate1_w)])),
        "shared_in": cut(np.concatenate([np.asarray(L0_ffn_sh_gate_w), np.asarray(L0_ffn_sh_up_w)])),
        "shared_out": np.asarray(L0_ffn_sh_down_w).T,
        "w_gu": np.asarray(L0_ffn_gu_w).reshape(E, 2 * I, CJ, P).transpose(0, 3, 2, 1),
        "w_dp": np.asarray(L0_ffn_dp_w).transpose(0, 2, 1),
    }
    arrays.update(shape_constants())
    return {k: np.ascontiguousarray(v) for k, v in arrays.items()}


def kernel(**inputs):
    import concourse.bacc as _bacc
    from concourse.bass_utils import run_bass_kernel_spmd as _run

    nc = _bacc.Bacc("TRN2", target_bir_lowering=False, num_devices=1)
    arrays = lay_out(**inputs)
    aps = {n: nc.dram_tensor(f"in_{n}", v.shape, mybir.dt.from_np(v.dtype), kind="ExternalInput").ap()
           for n, v in arrays.items()}
    out = nc.dram_tensor("out", [B * S + CAP, C], F32, kind="ExternalOutput").ap()
    build(nc, aps, out)
    r = _run(nc, [{f"in_{n}": v for n, v in arrays.items()}], core_ids=[0])
    return np.asarray(r.results[0]["out"])[:B * S].reshape(B, S, C)
```

```python
from contextlib import ExitStack

import numpy as np

import concourse.bass as bass
from concourse import mybir

F32 = mybir.dt.float32
F32R = mybir.dt.float32r
I32 = mybir.dt.int32
U32 = mybir.dt.uint32
ALU = mybir.AluOpType
ACT = mybir.ActivationFunctionType
AX_X = mybir.AxisListType.X

B, S, C = 16, 112, 512
L, D = 375, 128
H, K, Q, R = 16, 128, 384, 64
E, I, TOP = 64, 128, 8
EPS = 1e-5

P = 128
CJ = C // P
QC = 4
QW = Q // QC
LJ, LP = 3, L // 3
GB = 4
NG = B // GB
GT = GB * S
ROWS = H * S
RT = ROWS // P

TR = 96
MT = 3
CAP = TR * MT
ROUNDS = -(-(B * S - CAP) // TR)
STATIC = E * CAP
ENTRIES = STATIC + E * ROUNDS * TR
RING = 4
ROUND = 1.5 * 2 ** 23


def rope_tables(length, dim):
    inv = (1.0 / np.float32(10000.0) ** (np.arange(0, dim, 2, dtype=np.float32) / np.float32(dim))).astype(np.float32)
    f = (np.arange(length, dtype=np.float32)[:, None] * inv[None, :]).astype(np.float32)
    sin = np.repeat(np.sin(f), 2, axis=-1).astype(np.float32)
    cos = np.repeat(np.cos(f), 2, axis=-1).astype(np.float32)
    return sin, cos


def shape_constants():
    sq, cq = rope_tables(S, Q)
    sk, ck = rope_tables(L, D)
    half = Q // 2
    sr = np.concatenate([-sq[:, :half], sq[:, half:]], axis=1)
    skn = np.concatenate([-sk[:, :D // 2], sk[:, D // 2:]], axis=1)
    qt = lambda a: np.ascontiguousarray(a.T.reshape(QC, QW, S).transpose(1, 0, 2))
    lt = lambda a: np.ascontiguousarray(a.reshape(LJ, LP, D).transpose(1, 0, 2))
    tri = np.triu(np.ones((S, S), np.float32), 1)
    return {
        "c_cos_q": qt(cq), "c_sin_q": qt(sr), "c_cos_k": lt(ck), "c_sin_k": lt(skn),
        "c_ident": np.eye(P, dtype=np.float32),
        "c_before": tri,
        "c_ones": np.ones((S, P), np.float32),
        "c_expert": np.tile(np.arange(E, dtype=np.float32), (S, 1)),
        "c_token": np.ascontiguousarray(np.arange(B * S, dtype=np.float32).reshape(B, S).T),
        "c_minus_half": np.full((P, 1), -0.5, np.float32),
        "c_table": np.stack([B * S + np.arange(ENTRIES, dtype=np.float32) % CAP,
                             np.zeros(ENTRIES, np.float32)], axis=1),
        "c_expert_entries": np.tile(np.arange(E, dtype=np.float32) * CAP, (S, 1)),
        "c_expert_behind": np.tile(STATIC - CAP + np.arange(E, dtype=np.float32) * (ROUNDS * TR - CAP), (S, 1)),
        "c_pad_rows": np.zeros((CAP, C), np.float32),
    }


class Queue:

    def __init__(self, counts):
        self.ops, self.counts, self.passed = [], counts, {}

    def wait(self, *marks):
        for mark in marks:
            if mark is None:
                continue
            sem, value = mark
            if self.passed.get(id(sem), 0) < value:
                self.passed[id(sem)] = value
                self.ops.append(lambda eng, s=sem, v=value: eng.wait_ge(s, v))

    def do(self, fn, sem=None, by=1):
        if sem is None:
            self.ops.append(lambda eng: fn(eng))
            return None
        self.counts[id(sem)] = self.counts.get(id(sem), 0) + by
        self.ops.append(lambda eng: fn(eng).then_inc(sem, by))
        return sem, self.counts[id(sem)]

    def play(self, eng):
        for op in self.ops:
            op(eng)


def build(nc, a, out):
    with ExitStack() as ctx:
        def sb(name, shape, dt=F32):
            return ctx.enter_context(nc.sbuf_tensor(name, shape, dt))

        def sem(name):
            return ctx.enter_context(nc.semaphore(name))

        counts = {}
        pe, dve, act, pool, sp = (Queue(counts) for _ in range(5))

        bank = [ctx.enter_context(nc.psum_tensor(f"bank{i}", [P, 512], F32)) for i in range(8)]
        bank_read = [None] * 8

        m_dram = nc.dram_tensor("m_dram", [H, QW, QC * D], F32).ap()
        v_dram = nc.dram_tensor("v_dram", [H, D, C], F32).ap()
        xn2_dram = nc.dram_tensor("xn2_dram", [B * S + CAP, C], F32).ap()
        table = nc.dram_tensor("table", [ENTRIES, 2], F32).ap()

        cos_q = sb("cos_q", [QW, QC, S])
        sin_q = sb("sin_q", [QW, QC, S])
        cos_k = sb("cos_k", [LP, LJ, D])
        sin_k = sb("sin_k", [LP, LJ, D])
        ident = sb("ident", [P, P])
        before = sb("before", [S, S])
        ones = sb("ones", [S, P])
        expert = sb("expert", [S, E])
        token = sb("token", [S, B])
        expert_entries = sb("expert_entries", [S, E])
        expert_behind = sb("expert_behind", [S, E])
        minus_half = sb("minus_half", [P, 1])
        gates = sb("gates", [P, 2])
        tanh_g = sb("tanh_g", [P, 2])
        token_w = sb("token_w", [P, CJ, E + 1 + 2 * I])
        shared_out = sb("shared_out", [I, C])

        s_first = sem("s_first")
        s_const = sem("s_const")
        s_late = sem("s_late")
        s_zero = sem("s_zero")
        s_tanh = sem("s_tanh")
        s_pad = sem("s_pad")

        def load_constants(pairs, signal):
            for dst, src in pairs:
                mark = sp.do(lambda e, d=dst, s=src: e.dma_start(d, s), signal, 16)
            return mark

        first_loaded = load_constants([(ident[:], a["c_ident"]), (minus_half[:], a["c_minus_half"])], s_first)

        def load_rope_tables():
            return load_constants([(cos_q[:], a["c_cos_q"]), (sin_q[:], a["c_sin_q"]),
                                   (cos_k[:], a["c_cos_k"]), (sin_k[:], a["c_sin_k"])], s_const)

        def load_late_constants():
            return load_constants([
                (gates[:, 0:1], a["g_xattn"].partition_broadcast(P)), (gates[:, 1:2], a["g_ffn"].partition_broadcast(P)),
                (before[:], a["c_before"]), (ones[:], a["c_ones"]), (expert[:], a["c_expert"]), (token[:], a["c_token"]),
                (expert_entries[:], a["c_expert_entries"]),
                (expert_behind[:], a["c_expert_behind"]), (token_w[:], a["token_w"]),
                (shared_out[:], a["shared_out"])], s_late), load_constants([
                    (table, a["c_table"]), (xn2_dram[B * S:, :], a["c_pad_rows"]), (out[B * S:, :], a["c_pad_rows"])],
                    s_zero)

        m_stored, v_stored = [], []
        NF = 6
        NO = 4
        s_fold_qr = sem("s_fold_qr")
        s_fold_kv = sem("s_fold_kv")
        s_fold = sem("s_fold")
        s_fold_v = sem("s_fold_v")
        s_fold_a = sem("s_fold_a")
        s_st = [sem(f"s_fold_st{i}") for i in range(NF)]
        s_v_ld = [sem(f"s_v_ld{i}") for i in range(NO)]
        wo_loaded, v_done = [], []

        def load_fold_weights():
            for dst, src in ((wqr[:], a["w_qr"]), (wkr[:], a["w_kr"])):
                qr_loaded = act.do(lambda e, d=dst, s=src: e.dma_start(d, s), s_fold_qr, 16)
            return qr_loaded, act.do(lambda e: e.dma_start(wkv[:], a["w_kv"]), s_fold_kv, 16)

        def load_wo(h):
            sp.wait(v_done[h - NO] if h >= NO else None)
            wo_loaded.append(sp.do(lambda e: e.dma_start(wo[:, h % NO, :], a["w_o"][h]), s_v_ld[h % NO], 16))

        def fold_m(qr_loaded):
            pe.wait(qr_loaded)
            for h in range(H):
                bk = h % 8
                pe.wait(bank_read[bk])
                for c in range(QC):
                    m_ready = pe.do(lambda e, h=h, c=c, bk=bk: e.matmul(
                        bank[bk][0:QW, c * D:(c + 1) * D], wqr[:, h, c * QW:(c + 1) * QW], wkr[:, h, :],
                        start=True, stop=True), s_fold)
                (dve if h % 2 else act).wait(m_ready, m_stored[h - NF] if h >= NF else None)
                slot = folded[h % NF][0:QW, :]
                if h % 2:
                    done = dve.do(lambda e, bk=bk, o=slot: e.tensor_copy(o, bank[bk][0:QW, :]), s_fold_v)
                else:
                    done = act.do(lambda e, bk=bk, o=slot: e.activation(o, bank[bk][0:QW, :], ACT.Copy), s_fold_a)
                bank_read[bk] = done
                sp.wait(done)
                m_stored.append(sp.do(lambda e, h=h, i=slot: e.dma_start(m_dram[h], i), s_st[h % NF], 16))

        def fold_v(kv_loaded):
            pe.wait(kv_loaded)
            for h in range(H):
                bk = h % 8
                pe.wait(wo_loaded[h], bank_read[bk])
                v_done.append(pe.do(lambda e, h=h, bk=bk: e.matmul(bank[bk][:], wkv[:, h, :], wo[:, h % NO, :],
                                                                   start=True, stop=True), s_fold))
                if h + NO < H:
                    load_wo(h + NO)
                n = H + h
                slot, free = folded[n % NF], (m_stored + v_stored)[n - NF]
                if h % 2:
                    dve.wait(v_done[-1], free)
                    copied = dve.do(lambda e, bk=bk, o=slot: e.tensor_copy(o[:], bank[bk][:]), s_fold_v)
                else:
                    act.wait(v_done[-1], free)
                    copied = act.do(lambda e, bk=bk, o=slot: e.activation(o[:], bank[bk][:], ACT.Copy), s_fold_a)
                bank_read[bk] = copied
                act.wait(copied)
                v_stored.append(act.do(lambda e, h=h, i=slot: e.dma_start(v_dram[h], i[:]), s_st[n % NF], 16))
            return v_stored[-NF:]


        count = sb("count", [S, E])
        rounds = sb("rounds", [1, 1], I32)
        kept_sb = sb
        att_ctx = ExitStack()

        def sb(name, shape, dt=F32):
            return att_ctx.enter_context(nc.sbuf_tensor(name, shape, dt))

        NW = 2
        wq = [sb(f"wq{i}", [P, CJ, K]) for i in range(NW)]
        wcq = [sb(f"wcq{i}", [K, Q]) for i in range(NW)]
        m_w = [sb(f"m_w{i}", [QW, QC, D]) for i in range(NW)]
        wq_s = [[sb(f"wq_s{i}{p}", [P, CJ, K], F32R) for p in "hl"] for i in range(2)]
        wcq_s = [[sb(f"wcq_s{i}{p}", [K, Q], F32R) for p in "hl"] for i in range(2)]
        V_PASSES = NG + 1
        NV = 4
        v_raw = [sb(f"v_raw{i}", [D, C]) for i in range(NV)]
        v_w = [[sb(f"v_w{i}{p}", [D, C], F32R) for p in "hl"] for i in range(2)]
        xn_t = [sb(f"xn_t{p}", [P, CJ, GB, S], F32R) for p in "hl"]
        NX = 2 * GB
        x_sb = [sb(f"x_sb{i}", [S, C]) for i in range(NX)]
        kv_raw = sb("kv_raw", [LP, LJ, D])
        kv_tmp = sb("kv_tmp", [LP, LJ, D])
        kv_full = sb("kv_full", [LP, LJ, D])
        kv_r = [[sb(f"kv_r{i}{p}", [LP, LJ, D], F32R) for p in "hl"] for i in range(2)]
        kv_t = [[sb(f"kv_t{i}{p}", [D, L + 1], F32R) for p in "hl"] for i in range(2)]
        dve.wait(first_loaded)
        for part in (*kv_t[0], *kv_t[1]):
            dve.do(lambda e, o=part: e.tensor_scalar(o[:, L:L + 1], ident[:, 0:1], 0.0, None, ALU.mult), s_pad)
        NP = 4
        row_max = sb("row_max", [P, NP])
        row_sum = sb("row_sum", [P, NP])
        row_inv = sb("row_inv", [P, NP])
        xn1 = [sb(f"xn1{i}", [S, C]) for i in range(2)]
        xn2 = sb("xn2", [S, C])
        xn2_t = sb("xn2_t", [P, CJ, S])
        ln_stats = [sb(f"ln_stats{i}", [S, 16]) for i in range(GB + 1)]
        logit = sb("logit", [S, E + 1])
        left = sb("left", [S, E])
        mask = sb("mask", [S, E])
        rank_sb = sb("rank_sb", [S, E])
        behind = sb("behind", [S, E])
        scratch_e = sb("scratch_e", [S, TOP, E])
        top = sb("top", [S, TOP])
        top_i = sb("top_i", [S, TOP], U32)
        pair = sb("pair", [S, 3, TOP])
        pos_i = [sb(f"pos_i{i}", [S, TOP], I32) for i in range(2)]
        entry = [sb(f"entry{i}", [S, TOP, 2]) for i in range(2)]
        small = sb("small", [S, 8])
        sh_t = sb("sh_t", [S, I])
        sh_v = sb("sh_v", [S, I])
        sh_w = sb("sh_w", [S, I])
        sh_wt = sb("sh_wt", [I, S])
        with ExitStack() as turn_ctx:
            def turn_sb(name, shape, dt=F32):
                return turn_ctx.enter_context(nc.sbuf_tensor(name, shape, dt))

            q_hk = [[turn_sb(f"q_hk{i}{p}", [K, GT], F32R) for p in "hl"] for i in range(2)]
            q_rope = [turn_sb(f"q_rope{i}", [QW, QC, GT]) for i in range(2)]
            q_sin = turn_sb("q_sin", [QW, QC, GT])
        prob = [sb(f"prob{i}", [P, L]) for i in range(NP)]
        TB = 4
        prob_t = [[sb(f"prob_t{i}{p}", [LP, LJ, TB * P], F32R) for p in "hl"] for i in range(2)]
        with ExitStack() as fold:
            def fsb(name, shape, dt=F32):
                return fold.enter_context(nc.sbuf_tensor(name, shape, dt))

            wqr = fsb("wqr", [R, H, Q])
            wkr = fsb("wkr", [R, H, D])
            wkv = fsb("wkv", [K, H, D])
            folded = [fsb(f"folded{i}", [P, C]) for i in range(NF)]
            wo = fsb("wo", [K, NO, C])
        q_t = [sb(f"q_t{p}", [D, GB, H, S], F32R) for p in "hl"]

        s_x = [sem(f"s_x{i}") for i in range(NX)]
        s_w = {kind: [sem(f"s_{kind}{i}") for i in range(NW)] for kind in ("wq", "wcq", "m_w")}
        s_vl = [sem(f"s_vl{i}") for i in range(NV)]
        s_v_high = sem("s_v_high")
        s_v_low = sem("s_v_low")
        s_kv = sem("s_kv")
        s_ln = sem("s_ln")
        s_rstd = sem("s_rstd")
        s_xt = sem("s_xt")
        s_xt_ev = sem("s_xt_ev")
        s_qp = sem("s_qp")
        s_qp_ev = sem("s_qp_ev")
        s_ql = sem("s_ql")
        s_rope = sem("s_rope")
        s_rope_add = sem("s_rope_add")
        s_xt_low = sem("s_xt_low")
        s_hk_low = sem("s_hk_low")
        s_w_high = sem("s_w_high")
        s_w_low = {kind: sem(f"s_{kind}_low") for kind in ("wq", "wcq")}
        s_qd = sem("s_qd")
        s_qd_high = sem("s_qd_high")
        s_qd_low = sem("s_qd_low")
        s_krope = sem("s_krope")
        s_kt = sem("s_kt")
        s_kt_high = sem("s_kt_high")
        s_kt_low = sem("s_kt_low")
        s_score = sem("s_score")
        s_max = sem("s_max")
        s_exp = sem("s_exp")
        s_inv = sem("s_inv")
        s_norm = [sem(f"s_norm{i}") for i in range(3)]
        s_pt = sem("s_pt")
        s_pt_high = sem("s_pt_high")
        s_pt_low = sem("s_pt_low")
        s_ctx = sem("s_ctx")
        s_ctx_high = sem("s_ctx_high")
        s_ctx_low = sem("s_ctx_low")
        s_o = sem("s_o")
        s_x2 = sem("s_x2_made")
        s_route = sem("s_route")
        s_sh = sem("s_sh")
        s_sh_a = sem("s_sh_a")
        s_xn2_st = sem("s_xn2_st")
        s_base_st = sem("s_base_st")
        s_tab = [sem(f"s_tab{i}") for i in range(2)]

        def products(out_ap, weights, moving, first, last, signal):
            (wh, wl), (mh, ml) = weights, moving
            for n, (w, m) in enumerate(((wh, mh), (wh, ml), (wl, mh))):
                mark = pe.do(lambda e, w=w, m=m, n=n: e.matmul(out_ap, w, m, start=first and n == 0,
                                                               stop=last and n == 2), signal)
            return mark

        x_loaded = [None] * B
        x_used = [None] * B
        xt_ready = [None] * B
        xt_mm = [None] * B
        ln_ready = {}
        ln_used = [None] * (GB + 1)
        q_proj_over = None

        def layer_norm_stats(x_in, i):
            st, mv, rs = ln_stats[i][:, 0:6], ln_stats[i][:, 6:8], ln_stats[i][:, 0:1]
            dve.wait(ln_used[i])
            dve.wait(dve.do(lambda e: e.bn_stats(st, x_in), s_ln))
            pool.wait(dve.do(lambda e: e.bn_aggr(mv, st), s_ln))
            pool.wait(pool.do(lambda e: e.tensor_scalar(rs, mv[:, 1:2], EPS, None, ALU.add), s_rstd))
            return pool.do(lambda e: e.tensor_tensor(rs, rs, minus_half[0:S, :], ALU.pow), s_rstd)

        def layer_norm_apply(x_in, x_out, i, ready):
            mv, rs = ln_stats[i][:, 6:8], ln_stats[i][:, 0:1]
            dve.wait(ready)
            ln_used[i] = dve.do(lambda e: e.tensor_scalar(x_out, x_in, mv[:, 0:1], rs, ALU.subtract, ALU.mult), s_ln)
            return ln_used[i]

        def load_x(b):
            if b >= NX:
                sp.wait(x_used[b - NX])
            x_loaded[b] = sp.do(lambda e: e.dma_start(x_sb[b % NX][:], a["x"][b * S:(b + 1) * S, :]),
                                s_x[b % NX], 16)

        def stats_slot(b):
            return b if b < GB else GB

        def stats_x(b):
            dve.wait(x_loaded[b])
            ln_ready[b] = layer_norm_stats(x_sb[b % NX][:], stats_slot(b))

        def norm_x(b):
            dve.wait(xt_mm[b - 2] if b >= 2 else None)
            ln_ready[b] = layer_norm_apply(x_sb[b % NX][:], xn1[b % 2][:], stats_slot(b), ln_ready[b])

        def turn_x(b):
            pe.wait(ln_ready[b], bank_read[7])
            for j in range(CJ):
                t = pe.do(lambda e, j=j: e.transpose(bank[7][:, j * S:(j + 1) * S], xn1[b % 2][:, j * P:(j + 1) * P],
                                                     ident[0:S, 0:S]), s_xt)
            xt_mm[b] = t
            act.wait(t, q_proj_over)
            src = bank[7][:, 0:CJ * S].rearrange("p (j s) -> p j s", j=CJ)
            high, low = (x[:, :, b % GB, :] for x in xn_t)
            h = act.do(lambda e: e.activation(high, src, ACT.Copy), s_xt_ev)
            dve.wait(h)
            xt_ready[b] = bank_read[7] = dve.do(lambda e: e.tensor_tensor(low, src, high, ALU.subtract), s_xt_low)

        q_sin_free = {}
        kinds = ("wq", "wcq", "m_w")
        w_loaded = {kind: {} for kind in kinds}
        w_used = {kind: {} for kind in kinds}
        w_split = {kind: {} for kind in kinds}

        def load_weight(kind, n):
            if n >= NG * H:
                return
            h, i = n % H, n % NW
            dst, src = {"wq": (wq[i][:], a["w_q"][h]), "wcq": (wcq[i][:], a["w_cq"][h]),
                        "m_w": (m_w[i][:], m_dram[h].rearrange("p (c d) -> p c d", d=D))}[kind]
            sp.wait((w_used if kind == "m_w" else w_split)[kind].get(n - NW), m_stored[h] if kind == "m_w" else None)
            w_loaded[kind][n] = sp.do(lambda e: e.dma_start(dst, src), s_w[kind][i], 16)

        def split_weight(kind, n):
            if n >= NG * H:
                return
            full = {"wq": wq, "wcq": wcq}[kind][n % NW]
            high, low = {"wq": wq_s, "wcq": wcq_s}[kind][n % 2]
            act.wait(w_loaded[kind][n], w_used[kind].get(n - 2))
            h = act.do(lambda e: e.activation(high[:], full[:], ACT.Copy), s_w_high)
            queue = {"wq": pool, "wcq": dve}[kind]
            queue.wait(h)
            w_split[kind][n] = queue.do(lambda e: e.tensor_tensor(low[:], full[:], high[:], ALU.subtract), s_w_low[kind])
            load_weight(kind, n + NW)

        def query_phase(g, between):
            nonlocal q_proj_over
            hk_ready, rope_done, ql_done, qd_done, made = {}, {}, {}, {}, {}

            def project(h):
                n = g * H + h
                pe.wait(w_split["wq"][n], bank_read[0], *[xt_ready[g * GB + i] for i in range(GB)])
                for j in range(CJ):
                    m = products(bank[0][:, 0:GT], [w[:, j, :] for w in wq_s[n % 2]],
                                 [x[:, j, :, :].rearrange("p b s -> p (b s)") for x in xn_t], j == 0, j == CJ - 1, s_qp)
                w_used["wq"][n] = m
                high, low = q_hk[h % 2]
                act.wait(m, ql_done.get(h - 2))
                up = act.do(lambda e: e.activation(high[:], bank[0][:, 0:GT], ACT.Copy), s_qp_ev)
                dve.wait(up)
                hk_ready[h] = bank_read[0] = dve.do(lambda e: e.tensor_tensor(low[:], bank[0][:, 0:GT], high[:],
                                                                              ALU.subtract), s_hk_low)
                return m

            def latent(h):
                n = g * H + h
                pe.wait(w_split["wcq"][n], hk_ready[h])
                ready, order = {}, (0, 2, 1, 3)
                for c in order:
                    pe.wait(bank_read[1 + c])
                    ready[c] = m = (products(bank[1 + c][0:QW, 0:GT], [w[:, c * QW:(c + 1) * QW] for w in wcq_s[n % 2]],
                                          [x[:] for x in q_hk[h % 2]], True, True, s_ql))
                ql_done[h] = w_used["wcq"][n] = m
                for c in order:
                    dve.wait(ready[c], qd_done.get(h - 2), q_sin_free.get((c + QC // 2) % QC))
                    src = bank[1 + c][0:QW, 0:GT].rearrange("p (b s) -> p b s", b=GB)
                    for dst, tab, to in ((q_rope[h % 2], cos_q, c), (q_sin, sin_q, (c + QC // 2) % QC)):
                        r = dve.do(lambda e, d=dst, t=tab, to=to, src=src: e.tensor_tensor(
                            d[:, to, :].rearrange("p (b s) -> p b s", b=GB), src,
                            t[:, to, :].unsqueeze(1).to_broadcast([QW, GB, S]), ALU.mult), s_rope)
                    bank_read[1 + c] = made[c] = r
                for c in order:
                    pool.wait(made[c], made[(c + QC // 2) % QC])
                    q_sin_free[c] = pool.do(lambda e, c=c, o=q_rope[h % 2]: e.tensor_tensor(
                        o[:, c, :], o[:, c, :], q_sin[:, c, :], ALU.add), s_rope_add)
                    rope_done[h, c] = q_sin_free[c]

            def to_context(h):
                n = g * H + h
                pe.wait(w_loaded["m_w"][n], bank_read[5])
                for n_c, c in enumerate((0, 2, 1, 3)):
                    pe.wait(rope_done[h, c])
                    m = pe.do(lambda e, c=c, n_c=n_c: e.matmul(
                        bank[5][:, 0:GT], m_w[n % NW][:, c, :], q_rope[h % 2][:, c, :],
                        start=(n_c == 0), stop=(n_c == QC - 1)), s_qd)
                qd_done[h] = w_used["m_w"][n] = m
                src = bank[5][:, 0:GT].rearrange("p (b s) -> p b s", b=GB)
                act.wait(m, *q_t_free)
                high = act.do(lambda e: e.activation(q_t[0][:, :, h, :], src, ACT.Copy), s_qd_high)
                dve.wait(high)
                mark = bank_read[5] = dve.do(lambda e: e.tensor_tensor(q_t[1][:, :, h, :], src, q_t[0][:, :, h, :],
                                                                       ALU.subtract), s_qd_low)
                return mark

            for h in range(H + 2):
                if h < H:
                    split_weight("wq", g * H + h + 1)
                    split_weight("wcq", g * H + h)
                    last = project(h)
                if 1 <= h <= H:
                    latent(h - 1)
                for fn in between.get(2 * h, ()):
                    fn()
                if h >= 2:
                    q_ready = to_context(h - 2)
                if h >= 2:
                    load_weight("m_w", g * H + h - 2 + NW)
                for fn in between.get(2 * h + 1, ()):
                    fn()
            q_proj_over = last
            return q_ready

        q_t_free = []
        kv_ready = [None] * B
        kvr_ready = [None] * B
        kv_used = [None] * B
        krope_free = [None]
        scores_over = [None] * B

        def rope_context(b):
            i = b % 2
            sp.wait(krope_free[0])
            loaded = sp.do(lambda e: e.dma_start(kv_raw[:], a["ctx"][b].rearrange("(j p) d -> p j d", p=LP)), s_kv, 16)
            dve.wait(loaded, tables_loaded, kv_turned[0])
            hd = D // 2
            dve.do(lambda e: e.tensor_tensor(kv_full[:], kv_raw[:], cos_k[:], ALU.mult), s_krope)
            dve.do(lambda e: e.tensor_tensor(kv_tmp[:, :, 0:hd], kv_raw[:, :, hd:D], sin_k[:, :, 0:hd], ALU.mult), s_krope)
            m = dve.do(lambda e: e.tensor_tensor(kv_tmp[:, :, hd:D], kv_raw[:, :, 0:hd], sin_k[:, :, hd:D], ALU.mult),
                        s_krope)
            krope_free[0] = m
            dve.wait(m)
            f = dve.do(lambda e: e.tensor_tensor(kv_full[:], kv_full[:], kv_tmp[:], ALU.add), s_krope)
            dve.wait(f, kv_used[b - 2] if b >= 2 else None)
            high, low = kv_r[i]
            dve.wait(dve.do(lambda e: e.tensor_copy(high[:], kv_full[:]), s_krope))
            kvr_ready[b] = dve.do(lambda e: e.tensor_tensor(low[:], kv_full[:], high[:], ALU.subtract), s_krope)

        kv_turned = [None]

        def turn_context(b):
            pe.wait(kvr_ready[b], bank_read[7])
            for j in range(LJ):
                t = pe.do(lambda e, j=j: e.transpose(bank[7][:, j * LP:(j + 1) * LP], kv_full[:, j, :],
                                                     ident[0:LP, 0:LP]), s_kt)
            kv_turned[0] = t
            high, low = kv_t[b % 2]
            act.wait(t, scores_over[b - 2] if b >= 2 else None)
            h = act.do(lambda e: e.activation(high[:, 0:L], bank[7][:, 0:L], ACT.Copy), s_kt_high)
            dve.wait(h)
            kv_ready[b] = bank_read[7] = dve.do(lambda e: e.tensor_tensor(low[:, 0:L], bank[7][:, 0:L], high[:, 0:L],
                                                                          ALU.subtract), s_kt_low)

        tile_norm, pt_read, exp_done, pt_mm = {}, {}, {}, {}
        ctx_mm = {}
        ctx_ev = {}
        NBK = -(-RT // TB)

        def score_tile(b, t, q_ready):
            n = b * RT + t
            bk, i = n % 3, n % NP
            pe.wait(q_ready, kv_ready[b], bank_read[bk])
            rows = [q[:, b % GB, :, :].rearrange("d h s -> d (h s)")[:, t * P:(t + 1) * P] for q in q_t]
            m = scores_over[b] = products(bank[bk][:, 0:L + 1], rows, [k[:] for k in kv_t[b % 2]], True, True, s_score)
            dve.wait(m, exp_done.get(n - NP))
            mx = dve.do(lambda e: e.tensor_reduce(row_max[:, i:i + 1], bank[bk][:, 0:L], AX_X, ALU.max, negate=True), s_max)
            max_done[n] = mx

        def exponentials(b, t):
            n = b * RT + t
            bk, i = n % 3, n % NP
            act.wait(max_done[n], pt_mm.get(n - NP), inv_done.get(n - NP))
            exp_done[n] = bank_read[bk] = act.do(
                lambda e: e.activation(prob[i][:], bank[bk][:, 0:L], ACT.Exp, bias=row_max[:, i:i + 1],
                                       accum_out=row_sum[:, i:i + 1]), s_exp)

        inv_done, max_done = {}, {}
        finishing = []

        def reciprocals(b, t):
            n = b * RT + t
            i = n % NP
            dve.wait(exp_done[n], tile_norm.get(n - NP))
            inv_done[n] = dve.do(lambda e: e.reciprocal(row_inv[:, i:i + 1], row_sum[:, i:i + 1]), s_inv)

        def normalise(b, t):
            n = b * RT + t
            i = n % NP
            if n % 2:
                queue, signal = (dve, s_norm[2]) if finishing else (pool, s_norm[1])
                queue.wait(inv_done[n])
                tile_norm[n] = queue.do(lambda e: e.tensor_scalar(prob[i][:], prob[i][:], row_inv[:, i:i + 1], None,
                                                                  ALU.mult), signal)
            else:
                act.wait(inv_done[n])
                tile_norm[n] = act.do(lambda e: e.activation(prob[i][:], prob[i][:], ACT.Copy, scale=row_inv[:, i:i + 1]),
                                      s_norm[0])

        def turn_tile(b, t):
            n = b * RT + t
            i, bk = n % NP, 3 + n % 2
            blk = b * NBK + t // TB
            pe.wait(tile_norm[n], bank_read[bk])
            for j in range(LJ):
                m = pe.do(lambda e, j=j: e.transpose(bank[bk][0:LP, j * P:(j + 1) * P], prob[i][:, j * LP:(j + 1) * LP],
                                                     ident[:]), s_pt)
            pt_mm[n] = m

        def split_tile(b, t):
            n = b * RT + t
            bk = 3 + n % 2
            blk = b * NBK + t // TB
            src = bank[bk][0:LP, 0:LJ * P].rearrange("p (j r) -> p j r", j=LJ)
            high, low = (p[:, :, (t % TB) * P:(t % TB + 1) * P] for p in prob_t[blk % 2])
            act.wait(pt_mm[n], ctx_mm.get(blk - 2))
            h = act.do(lambda e: e.activation(high, src, ACT.Copy), s_pt_high)

            def split_low():
                dve.wait(h)
                pt_read[n] = bank_read[bk] = dve.do(lambda e: e.tensor_tensor(low, src, high, ALU.subtract), s_pt_low)
            return split_low

        def attend(b, blk):
            n, width = b * NBK + blk, min(TB, RT - TB * blk) * P
            bk = 5 + n % 2
            pe.wait(pt_read[b * RT + min(TB * blk + TB - 1, RT - 1)], kvr_ready[b], bank_read[bk])
            for j in range(LJ):
                m = products(bank[bk][:, 0:width], [k[:, j, :] for k in kv_r[b % 2]],
                             [p[:, j, 0:width] for p in prob_t[n % 2]], j == 0, j == LJ - 1, s_ctx)
            ctx_mm[n] = kv_used[b] = m
            return lambda: keep_context(b, blk, width, bk, m)

        def keep_context(b, blk, width, bk, m):
            at = blk * TB * P
            high, low = (q[:, b % GB, :, :].rearrange("d h s -> d (h s)")[:, at:at + width] for q in q_t)
            act.wait(m)
            h = act.do(lambda e: e.activation(high, bank[bk][:, 0:width], ACT.Copy), s_ctx_high)
            dve.wait(h)
            ctx_ev[b] = bank_read[bk] = dve.do(lambda e: e.tensor_tensor(low, bank[bk][:, 0:width], high, ALU.subtract),
                                               s_ctx_low)

        v_loaded, v_split, v_used = [], [], []

        def load_v(n):
            h, i = n % H, n % NV
            sp.wait(v_split[n - NV] if n >= NV else None, v_stored[h])
            v_loaded.append(sp.do(lambda e: e.dma_start(v_raw[i][:], v_dram[h]), s_vl[i], 16))

        def split_v(n):
            full, (high_part, low_part) = v_raw[n % NV], v_w[n % 2]
            act.wait(v_loaded[n], v_used[n - 2] if n >= 2 else None)
            high = act.do(lambda e: e.activation(high_part[:], full[:], ACT.Copy), s_v_high)
            dve.wait(high)
            v_split.append(dve.do(lambda e: e.tensor_tensor(low_part[:], full[:], high_part[:], ALU.subtract), s_v_low))
            if n + NV < V_PASSES * H:
                load_v(n + NV)

        def project_out(batches):
            pe.wait(*[ctx_ev[b] for b in batches], *[bank_read[4 + b % GB] for b in batches])
            for h in range(H):
                n = len(v_used)
                if h == 0:
                    split_v(n)
                if h + 1 < H:
                    split_v(n + 1)
                pe.wait(v_split[n])
                for i in (b % GB for b in batches):
                    m = products(bank[4 + i][0:S, :], [q[:, i, h, :] for q in q_t],
                                 [v[:] for v in v_w[n % 2]], h == 0, h == H - 1, s_o)
                v_used.append(m)
            q_t_free[:] = [m]
            for b in batches:
                x = x_sb[b % NX]
                dve.wait(m, tanh_done)
                r = bank_read[4 + b % GB] = dve.do(lambda e, b=b, x=x: e.scalar_tensor_tensor(
                    x[:], bank[4 + b % GB][0:S, :], tanh_g[0:S, 0:1], x[:], ALU.mult, ALU.add), s_x2)
                dve.wait(r)
                ln_ready[B + b] = layer_norm_stats(x[:], b % GB)

        base_done, xn2_turned, xn2_ready, xn2t_ready, sh_ready = [None], [None], [None], [None], [None]
        xn2t_used = [None]
        route_done = [None]
        xn2_stored, base_stored = [None], [None]
        scattered = [None, None]
        mask_used = [None]

        def norm_x2(b):
            dve.wait(xn2_stored[0], xn2_turned[0])
            xn2_ready[0] = n = layer_norm_apply(x_sb[b % NX][:], xn2[:], b % GB, ln_ready[B + b])
            sp.wait(n)
            xn2_stored[0] = sp.do(lambda e: e.dma_start(xn2_dram[b * S:(b + 1) * S, :], xn2[:]), s_xn2_st, 16)

        def turn_xn2(b):
            pe.wait(xn2_ready[0], bank_read[7])
            for j in range(CJ):
                m = pe.do(lambda e, j=j: e.transpose(bank[7][:, j * S:(j + 1) * S], xn2[:, j * P:(j + 1) * P],
                                                     ident[0:S, 0:S]), s_xt)
            xn2_turned[0] = m
            act.wait(m, xn2t_used[0])
            xn2t_ready[0] = bank_read[7] = act.do(
                lambda e: e.activation(xn2_t[:], bank[7][:, 0:CJ * S].rearrange("p (j s) -> p j s", j=CJ), ACT.Copy),
                s_xt_ev)

        def router_and_shared_in(b, bk):
            pe.wait(xn2t_ready[0], bank_read[bk])
            for j in range(CJ):
                m = pe.do(lambda e, j=j: e.matmul(bank[bk][0:S, 0:E + 1 + 2 * I], xn2_t[:, j, :], token_w[:, j, :],
                                                  start=(j == 0), stop=(j == CJ - 1)), s_sh)
            xn2t_used[0] = m
            return m

        def router_and_shared_results(b, bk, m):
            gate, up = (bank[bk][0:S, E + 1 + i * I:E + 1 + (i + 1) * I] for i in range(2))
            act.wait(m, base_done[0])
            act.do(lambda e: e.activation(sh_t[:], gate, ACT.Tanh, scale=0.5), s_sh_a)
            th = act.do(lambda e: e.activation(small[:, 0:1], bank[bk][0:S, E:E + 1], ACT.Tanh, scale=0.5), s_sh_a)
            dve.wait(th, route_done[0])
            dve.do(lambda e: e.tensor_copy(logit[:], bank[bk][0:S, 0:E + 1]), s_route)
            v = dve.do(lambda e: e.scalar_tensor_tensor(sh_v[:], sh_t[:], 1.0, gate, ALU.add, ALU.mult), s_route)
            dve.wait(v)
            sh_ready[0] = bank_read[bk] = dve.do(
                lambda e: e.scalar_tensor_tensor(sh_w[:], sh_v[:], 0.5, up, ALU.mult, ALU.mult), s_route)

        def shared_down(b, bk):
            pe.wait(sh_ready[0], bank_read[bk])
            m = pe.do(lambda e: e.transpose(bank[bk][:, 0:S], sh_w[:], ident[0:S, 0:S]), s_sh)
            act.wait(m, base_done[0])
            turned = act.do(lambda e: e.activation(sh_wt[:], bank[bk][:, 0:S], ACT.Copy), s_sh_a)
            pe.wait(turned)
            m = pe.do(lambda e: e.matmul(bank[bk][0:S, :], sh_wt[:], shared_out[:], start=True, stop=True), s_sh)
            dve.wait(m)
            dve.wait(dve.do(lambda e: e.tensor_scalar(small[:, 1:2], small[:, 0:1], 1.0, 0.5, ALU.add, ALU.mult), s_route))
            dve.wait(dve.do(lambda e: e.tensor_tensor(small[:, 2:3], small[:, 1:2], tanh_g[0:S, 1:2], ALU.mult), s_route))
            base_done[0] = bank_read[bk] = dve.do(lambda e: e.scalar_tensor_tensor(
                x_sb[b % NX][:], bank[bk][0:S, :], small[:, 2:3], x_sb[b % NX][:], ALU.mult, ALU.add), s_route)
            sp.wait(base_done[0])
            x_used[b] = base_stored[0] = sp.do(
                lambda e: e.dma_start(out[b * S:(b + 1) * S, :], x_sb[b % NX][:]), s_base_st, 16)

        def chain(fn):
            mark = dve.do(fn, s_route)
            dve.wait(mark)
            return mark

        def choose(b):
            lg = logit[:, 0:E]
            dve.wait((s_route, counts[id(s_route)]))
            if b == 0:
                dve.do(lambda e: e.memset(count[:], 0.0), s_route)
            chain(lambda e: e.max(top[:], lg))
            dve.do(lambda e: e.max_index(top_i[:], top[:], lg), s_route)
            chain(lambda e: e.match_replace(out=left[:], in_to_replace=top[:], in_values=lg, imm_value=-3.4028235e38))
            if mask_used[0] is not None:
                dve.wait(mask_used[0])
            mk = chain(lambda e: e.tensor_tensor(mask[:], left[:], lg, ALU.not_equal))
            dve.do(lambda e: e.tensor_copy(pair[:, 0, :], top_i[:]), s_route)
            mx = chain(lambda e: e.tensor_scalar(small[:, 3:4], top[:, 0:1], -1.0, None, ALU.mult))
            act.wait(mx)
            ex = act.do(lambda e: e.activation(pair[:, 1, :], top[:], ACT.Exp, bias=small[:, 3:4],
                                               accum_out=small[:, 4:5]), s_sh_a)
            pe.wait(mk, bank_read[7])
            pe.do(lambda e: e.matmul(bank[7][0:S, 0:E], before[:], mask[:], start=True, stop=False), s_sh)
            rank = pe.do(lambda e: e.matmul(bank[7][0:S, 0:E], ones[:, 0:S], count[:], start=False, stop=True), s_sh)
            dve.wait(ex)
            chain(lambda e: e.reciprocal(small[:, 5:6], small[:, 4:5]))
            chain(lambda e: e.tensor_tensor(small[:, 6:7], small[:, 5:6], tanh_g[0:S, 1:2], ALU.mult))
            dve.wait(scattered[b % 2])
            dve.do(lambda e: e.tensor_scalar(entry[b % 2][:, :, 1], pair[:, 1, :], small[:, 6:7], None, ALU.mult), s_route)
            dve.do(lambda e: e.tensor_copy(entry[b % 2][:, :, 0], token[:, b:b + 1].to_broadcast([S, TOP])), s_route)
            return rank

        def place(b, rank):
            dve.wait(rank)
            ranks = bank[7][0:S, 0:E]
            dve.do(lambda e: e.tensor_tensor(rank_sb[:], ranks, expert_entries[:], ALU.add), s_route)
            bank_read[7] = chain(lambda e: e.scalar_tensor_tensor(behind[:], ranks, float(CAP), expert_behind[:],
                                                                  ALU.is_ge, ALU.mult))
            chain(lambda e: e.tensor_tensor(rank_sb[:], rank_sb[:], behind[:], ALU.add))
            mask_used[0] = dve.do(lambda e: e.tensor_tensor(count[:], count[:], mask[:], ALU.add), s_route)
            for k in range(TOP):
                last = dve.do(lambda e, k=k: e.scalar_tensor_tensor(
                    scratch_e[:, k, :], expert[:], pair[:, 0, k:k + 1], rank_sb[:], ALU.is_equal, ALU.mult,
                    accum_out=pair[:, 2, k:k + 1]), s_route)
            dve.wait(last)
            route_done[0] = chain(lambda e: e.tensor_copy(pos_i[b % 2][:], pair[:, 2, :]))

        def scatter(b, ks):
            pool.wait(route_done[0], table_clear)
            for k in ks:
                scattered[b % 2] = pool.do(lambda e, k=k: e.indirect_dma_start(
                    table, bass.IndirectOffsetOnAxis(ap=pos_i[b % 2][:, k:k + 1], axis=0), entry[b % 2][:, k, :], None),
                    s_tab[b % 2], 16)

        for b in range(GB):
            load_x(b)
        fold_loaded = load_fold_weights()
        for kind in ("wq", "wcq"):
            for n in range(NW):
                load_weight(kind, n)
        tables_loaded = load_rope_tables()
        for h in range(NO):
            load_wo(h)
        for queue in (pe, pool):
            queue.wait(first_loaded)
        for b in range(GB):
            stats_x(b)
        norm_x(0)
        for b in range(GB):
            if b + 1 < GB:
                norm_x(b + 1)
            turn_x(b)
        split_weight("wq", 0)
        rope_context(0)
        fold_m(fold_loaded[0])
        for n in range(NW):
            load_weight("m_w", n)
        q_t_free[:] = fold_v(fold_loaded[1])
        turn_context(0)
        for n in range(NV):
            load_v(n)
        late_loaded, table_clear = load_late_constants()
        TURN_LAG = 4
        ATTEND_LAG = 2
        ALL_LAGS = TURN_LAG + ATTEND_LAG + 1

        chosen = []

        def finish_batch(b, bk=6):
            return [lambda: norm_x2(b),
                    lambda: turn_xn2(b),
                    lambda: router_and_shared_results(b, bk, router_and_shared_in(b, bk)),
                    lambda: chosen.append(choose(b)),
                    lambda: place(b, chosen.pop()),
                    lambda: shared_down(b, bk),
                    lambda: scatter(b, range(TOP // 2)),
                    lambda: scatter(b, range(TOP // 2, TOP))]

        between = {}
        HALF = GB // 2 * RT + ALL_LAGS
        for g in range(NG):
            q_ready = query_phase(g, between)
            if g == 0:
                for queue in (act, dve, pe):
                    queue.wait(late_loaded)
                tanh_done = act.do(lambda e: e.activation(tanh_g[:], gates[:], ACT.Tanh), s_tanh)
            tiles = [(b, i) for b in range(g * GB, (g + 1) * GB) for i in range(RT)]
            attend_due, evacuate_due = {}, []
            for t in range(len(tiles) + ALL_LAGS):
                if 0 <= t - 2 < len(tiles):
                    reciprocals(*tiles[t - 2])
                if t < len(tiles):
                    score_tile(*tiles[t], q_ready)
                if g == NG - 1 and t == HALF:
                    project_out(range(B - GB, B - GB // 2))
                    finishing.extend(step for b in range(B - GB, B - GB // 2) for step in finish_batch(b, 7))
                elif finishing and (t - HALF) % 2 == 1:
                    finishing.pop(0)()
                if 0 <= t - TURN_LAG < len(tiles):
                    turn_tile(*tiles[t - TURN_LAG])
                for evacuate in evacuate_due:
                    evacuate()
                evacuate_due = []
                for b, blk in attend_due.pop(t, ()):
                    evacuate_due.append(attend(b, blk))
                low = split_tile(*tiles[t - TURN_LAG]) if 0 <= t - TURN_LAG < len(tiles) else None
                if 0 <= t - 1 < len(tiles):
                    exponentials(*tiles[t - 1])
                if 0 <= t - 2 < len(tiles):
                    normalise(*tiles[t - 2])
                if low:
                    low()
                    b, i = tiles[t - TURN_LAG]
                    if i % TB == TB - 1 or i == RT - 1:
                        attend_due.setdefault(t + ATTEND_LAG, []).append((b, i // TB))
                if t < len(tiles):
                    b, i = tiles[t]
                    if b + 1 < B:
                        if i == 7:
                            rope_context(b + 1)
                        if i == 11:
                            turn_context(b + 1)
                    if b + GB < B:
                        if i == 0:
                            load_x(b + GB)
                        if i == 2:
                            stats_x(b + GB)
                        if i == 5:
                            norm_x(b + GB)
                        if i == 7:
                            turn_x(b + GB)
            last_group = g == NG - 1
            project_out(range(g * GB + (GB // 2 if last_group else 0), (g + 1) * GB))
            between = {}
            for b in range(0 if last_group else g * GB, 0 if last_group else (g + 1) * GB):
                steps = finish_batch(b)
                for at, step in zip((1, 3, 5, 7, 7, 9, 9, 11), steps):
                    between.setdefault(8 * (b % GB) + at, []).append(step)

        att_ctx.close()
        sb = kept_sb

        NE = 3
        w_gu = [sb(f"w_gu{i}", [P, CJ, 2 * I]) for i in range(NE)]
        w_dp = [sb(f"w_dp{i}", [I, C]) for i in range(NE)]
        w_gu_s = [[sb(f"w_gu_s{i}{p}", [P, CJ, 2 * I], F32R) for p in "hl"] for i in range(2)]
        w_dp_s = [[sb(f"w_dp_s{i}{p}", [I, C], F32R) for p in "hl"] for i in range(3)]
        NXG = RING * CAP // P
        x_g = [sb(f"x_g{i}", [P, C]) for i in range(NXG)]
        xg_t = [sb(f"xg_t{p}", [P, CJ, RING * CAP], F32R) for p in "hl"]
        e_tanh = [sb(f"e_tanh{i}", [I, CAP]) for i in range(2)]
        e_half = [sb(f"e_half{i}", [I, CAP]) for i in range(2)]
        e_inner = [sb(f"e_inner{i}", [I, CAP]) for i in range(2)]
        e_inner_s = [[sb(f"e_inner_s{i}{p}", [I, CAP], F32R) for p in "hl"] for i in range(2)]
        NY = 2 * MT
        y_sb = [sb(f"y_sb{i}", [TR, C]) for i in range(NY)]
        total = sb("total", [S, 4])
        GT_P, GT_R = STATIC // P, STATIC // TR
        rows_p = sb("rows_p", [GT_P // 2, 2, P, 2])
        rows_r = sb("rows_r", [GT_R // 2, 2, TR, 2])
        gather_t = sb("gather_t", [P, GT_P], I32)
        add_t = sb("add_t", [TR, GT_R], I32)
        add_w = sb("add_w", [TR, GT_R])

        s_ew = [sem(f"s_ew{i}") for i in range(NE)]
        s_ws_a = sem("s_ws_a")
        s_ws_v = sem("s_ws_v")
        s_index = sem("s_index")
        s_turned_index = sem("s_turned_index")
        s_xg = [sem(f"s_xg{i}") for i in range(NXG)]
        s_et = sem("s_et")
        s_et_a = sem("s_et_a")
        s_et_v = sem("s_et_v")
        s_gu = sem("s_gu")
        s_tanh_e = sem("s_tanh_e")
        s_inner = sem("s_inner")
        s_down = sem("s_down")
        s_y_a = sem("s_y_a")
        s_y_v = sem("s_y_v")
        s_add = [sem(f"s_add{i}") for i in range(NY)]
        s_rounds = sem("s_rounds")

        ew_loaded, ew_split, down_done, gathered, turned, gu_done, inner_done = {}, {}, {}, {}, {}, {}, {}
        xt_high, xt_low, y_ready, added = {}, {}, {}, {}

        def load_expert(x):
            sp.wait(ew_split.get(x - NE))
            for dst, src in ((w_gu[x % NE][:], a["w_gu"][x]), (w_dp[x % NE][:], a["w_dp"][x])):
                ew_loaded[x] = sp.do(lambda e, d=dst, s=src: e.dma_start(d, s), s_ew[x % NE], 16)

        sp.wait(*[used[NG * H - 1 - i] for used in (*w_used.values(), w_split["wq"], w_split["wcq"]) for i in range(2)])
        for x in range(NE):
            load_expert(x)
        for step in finishing:
            step()
        b = B - 2
        steps, last_steps = finish_batch(b, 6), finish_batch(b + 1, 5)
        for step in steps[:3] + last_steps[:2] + steps[3:6]:
            step()
        last_in = router_and_shared_in(b + 1, 5)
        for step in steps[6:]:
            step()
        router_and_shared_results(b + 1, 5, last_in)
        for step in last_steps[3:]:
            step()
        attention_over = [route_done[0], mask_used[0], *scattered, base_stored[0], xn2_stored[0]]
        for queue in (pe, dve, act, pool, sp):
            queue.wait(*attention_over)

        totals = pe.do(lambda e: e.matmul(bank[7][0:S, 0:E], ones[:, 0:S], count[:], start=True, stop=True), s_et)
        dve.wait(totals)
        for fn in (lambda e: e.tensor_reduce(total[:, 0:1], bank[7][0:S, 0:E], AX_X, ALU.max),
                   lambda e: e.tensor_scalar(total[:, 1:2], total[:, 0:1], (TR - 1) / 2 - CAP, 1.0 / TR, ALU.add, ALU.mult),
                   lambda e: e.tensor_scalar(total[:, 2:3], total[:, 1:2], ROUND, -ROUND, ALU.add, ALU.add),
                   lambda e: e.tensor_scalar(total[:, 3:4], total[:, 2:3], 0.0, float(ROUNDS), ALU.max, ALU.min),
                   lambda e: e.tensor_copy(rounds[:], total[0:1, 3:4])):
            rounds_ready = dve.do(fn, s_rounds)
            dve.wait(rounds_ready)
        bank_read[7] = rounds_ready

        for rows, m in ((rows_p, P), (rows_r, TR)):
            rows_loaded = sp.do(lambda e, rows=rows, m=m: e.dma_start(
                rows[:].rearrange("n g m w -> n g (m w)"),
                table[0:STATIC, :].rearrange("(g n m) w -> n g (m w)", g=2, m=m)), s_index, 16)
        pe.wait(rows_loaded)
        for g in range(2):
            n = GT_P // 2
            turned_p = pe.do(lambda e, g=g, n=n: e.transpose(bank[5][:, g * n:(g + 1) * n], rows_p[:, g, :, 0],
                                                             ident[0:n, 0:n]), s_et)
        for w in range(2):
            for g in range(2):
                n = GT_R // 2
                turned_r = pe.do(lambda e, g=g, w=w, n=n: e.transpose(
                    bank[6][0:TR, (2 * w + g) * n:(2 * w + g + 1) * n], rows_r[:, g, :, w], ident[0:n, 0:n]), s_et)
        dve.wait(turned_p)
        gather_ready = bank_read[5] = dve.do(lambda e: e.tensor_copy(gather_t[:], bank[5][:, 0:GT_P]), s_turned_index)
        dve.wait(turned_r)
        dve.do(lambda e: e.tensor_copy(add_t[:], bank[6][0:TR, 0:GT_R]), s_turned_index)
        add_ready = bank_read[6] = dve.do(lambda e: e.tensor_copy(add_w[:], bank[6][0:TR, GT_R:2 * GT_R]),
                                          s_turned_index)
        def split_expert(x):
            for full, (high, low), used in ((w_gu[x % NE], w_gu_s[x % 2], gu_done.get(x - 2)),
                                            (w_dp[x % NE], w_dp_s[x % 3], down_done.get(x - 3))):
                act.wait(ew_loaded[x], used)
                h = act.do(lambda e, o=high, i=full: e.activation(o[:], i[:], ACT.Copy), s_ws_a)
                dve.wait(h)
                ew_split[x] = dve.do(
                    lambda e, o=low, i=full, h=high: e.tensor_tensor(o[:], i[:], h[:], ALU.subtract), s_ws_v)

        def tiles_for(x):
            return range(-(-x * CAP // P), -(-(x + 1) * CAP // P))

        def gather(x):
            for n in tiles_for(x):
                pool.wait(gather_ready, turned.get(n - NXG))
                gathered[n] = pool.do(lambda e, n=n: e.indirect_dma_start(
                    x_g[n % NXG][:], None, xn2_dram, bass.IndirectOffsetOnAxis(ap=gather_t[:, n:n + 1], axis=0)),
                    s_xg[n % NXG], 16)

        def turn(x):
            for n in tiles_for(x):
                bk = n % 3
                pe.wait(gathered[n], bank_read[bk])
                for j in range(CJ):
                    m = pe.do(lambda e, n=n, j=j, bk=bk: e.transpose(
                        bank[bk][:, j * P:(j + 1) * P], x_g[n % NXG][:, j * P:(j + 1) * P], ident[:]), s_et)
                turned[n] = m
                src = bank[bk][:].rearrange("p (j t) -> p j t", j=CJ)
                high, low = (t[:, :, n % NXG * P:(n % NXG + 1) * P] for t in xg_t)
                act.wait(m, gu_done[((n - NXG + 1) * P - 1) // CAP] if n >= NXG else None)
                h = act.do(lambda e, src=src, high=high: e.activation(high, src, ACT.Copy), s_et_a)
                dve.wait(h)
                xt_low[x] = bank_read[bk] = dve.do(lambda e, src=src, high=high, low=low: e.tensor_tensor(
                    low, src, high, ALU.subtract), s_et_v)

        def inner(x):
            g, u = 3, 4
            pe.wait(ew_split[x], xt_low[x], bank_read[g], bank_read[u])
            for bk, at in ((g, 0), (u, I)):
                for j in range(CJ):
                    m = products(bank[bk][:, 0:CAP], [w[:, j, at:at + I] for w in w_gu_s[x % 2]],
                                 [t[:, j, x % RING * CAP:(x % RING + 1) * CAP] for t in xg_t], j == 0, j == CJ - 1,
                                 s_gu)
            gu_done[x] = m
            i = x % 2
            high, low = e_inner_s[i]
            act.wait(m, inner_done.get(x - 2))
            t = act.do(lambda e: e.activation(e_tanh[i][:], bank[g][:, 0:CAP], ACT.Tanh, scale=0.5), s_tanh_e)
            dve.wait(t, down_done.get(x - 2))
            v = dve.do(lambda e: e.scalar_tensor_tensor(e_half[i][:], e_tanh[i][:], 1.0, bank[g][:, 0:CAP], ALU.add,
                                                        ALU.mult), s_inner)
            dve.wait(v)
            w = bank_read[g] = bank_read[u] = dve.do(lambda e: e.scalar_tensor_tensor(
                e_inner[i][:], e_half[i][:], 0.5, bank[u][:, 0:CAP], ALU.mult, ALU.mult), s_inner)
            dve.wait(w)
            dve.wait(dve.do(lambda e: e.tensor_copy(high[:], e_inner[i][:]), s_inner))
            inner_done[x] = dve.do(lambda e: e.tensor_tensor(low[:], e_inner[i][:], high[:], ALU.subtract), s_inner)

        def down(x):
            for i in range(MT):
                n = x * MT + i
                bk = 5 + n % 3
                pe.wait(inner_done[x], bank_read[bk])
                m = products(bank[bk][0:TR, :], [w[:, i * TR:(i + 1) * TR] for w in e_inner_s[x % 2]],
                             [w[:] for w in w_dp_s[x % 3]], True, True, s_down)
                down_done[x] = m
                w = add_w[:, n:n + 1]
                if i % 2:
                    dve.wait(m, added.get(n - NY), add_ready)
                    r = dve.do(lambda e, n=n, bk=bk, w=w: e.tensor_scalar(y_sb[n % NY][:], bank[bk][0:TR, :], w, None,
                                                                          ALU.mult), s_y_v)
                else:
                    act.wait(m, added.get(n - NY), add_ready)
                    r = act.do(lambda e, n=n, bk=bk, w=w: e.activation(y_sb[n % NY][:], bank[bk][0:TR, :], ACT.Copy,
                                                                       scale=w), s_y_a)
                bank_read[bk] = y_ready[n] = r

        def add(x):
            if x:
                pool.wait(*[added[n] for n in range((x - 1) * MT, x * MT)])
            for n in range(x * MT, (x + 1) * MT):
                pool.wait(y_ready[n], add_ready)
                added[n] = pool.do(lambda e, n=n: e.indirect_dma_start(
                    out, bass.IndirectOffsetOnAxis(ap=add_t[:, n:n + 1], axis=0), y_sb[n % NY][:], None,
                    compute_op=ALU.add), s_add[n % NY], 16)

        for x in range(NE):
            gather(x)
        turn(0)
        split_expert(0)
        for x in range(E + 1):
            if x + 3 < E:
                load_expert(x + 3)
                gather(x + 3)
            if x + 1 < E:
                turn(x + 1)
                split_expert(x + 1)
            if x < E:
                inner(x)
            if x >= 1:
                down(x - 1)
                add(x - 1)
        adds_over = [added[n] for n in range((E - 1) * MT, E * MT)]

        lp = {n: sem(f"s_loop_{n}") for n in ("load", "token", "gather", "turn", "turned", "gu", "tanh", "half",
                                              "inner", "down", "y", "stored")}
        s_loop_gather = sem("s_loop_gather_dma")
        s_loop_add = sem("s_loop_add_dma")
        l_entry = sb("l_entry", [TR, 2])
        l_token = sb("l_token", [TR, 1], I32)
        l_xt = sb("l_xt", [P, CJ, TR])

        def take(eng, name, value=1):
            eng.wait_ge(lp[name], value)
            eng.sem_clear(lp[name])

        def loop(body):
            def run(eng):
                n = eng.value_load(rounds[0:1, 0:1], min_val=0, max_val=ROUNDS)
                with eng.If(n > 0):
                    with eng.Fori(0, n) as r:
                        with eng.Fori(0, E) as x:
                            body(eng, r, x)
            return run

        def loop_sp(eng, r, x):
            tile = STATIC // TR + x * ROUNDS + r
            eng.dma_start(w_gu[0][:], a["w_gu"][bass.ds(x, 1)].rearrange("one p j i -> p (one j) i"))\
               .then_inc(lp["load"], 16)
            eng.dma_start(w_dp[0][:], a["w_dp"][bass.ds(x, 1)].rearrange("one i c -> i (one c)")).then_inc(lp["load"], 16)
            eng.dma_start(l_entry[:], table.rearrange("(n m) w -> m n w", m=TR)[:, bass.ds(tile, 1), :]
                          .rearrange("m one w -> m (one w)"))\
               .then_inc(lp["load"], 16)
            take(eng, "stored")

        def loop_pool(eng, r, x):
            take(eng, "token")
            eng.indirect_dma_start(x_g[0][0:TR, :], None, xn2_dram, bass.IndirectOffsetOnAxis(ap=l_token[:], axis=0))\
               .then_inc(s_loop_gather, 16)
            eng.wait_ge(s_loop_gather, (r * E + x + 1) * 16)
            eng.nop().then_inc(lp["gather"], 1)
            take(eng, "y")
            eng.indirect_dma_start(out, bass.IndirectOffsetOnAxis(ap=l_token[:], axis=0), y_sb[0][:], None,
                                   compute_op=ALU.add).then_inc(s_loop_add, 16)
            eng.wait_ge(s_loop_add, (r * E + x + 1) * 16)
            eng.nop().then_inc(lp["stored"], 1)

        def loop_pe(eng, r, x):
            take(eng, "gather")
            for j in range(CJ):
                m = eng.transpose(bank[0][:, j * TR:(j + 1) * TR], x_g[0][0:TR, j * P:(j + 1) * P], ident[0:TR, 0:TR])
            m.then_inc(lp["turn"], 1)
            take(eng, "turned")
            for bk, at in ((2, 0), (3, I)):
                for j in range(CJ):
                    m = eng.matmul(bank[bk][:, 0:TR], w_gu[0][:, j, at:at + I], l_xt[:, j, :],
                                   start=(j == 0), stop=(j == CJ - 1))
            m.then_inc(lp["gu"], 1)
            take(eng, "inner")
            eng.matmul(bank[6][0:TR, :], e_inner[0][:, 0:TR], w_dp[0][:], start=True, stop=True).then_inc(lp["down"], 1)

        def loop_act(eng, r, x):
            take(eng, "turn")
            eng.activation(l_xt[:], bank[0][:, 0:CJ * TR].rearrange("p (j t) -> p j t", j=CJ), ACT.Copy)\
               .then_inc(lp["turned"], 1)
            take(eng, "gu")
            eng.activation(e_tanh[0][:, 0:TR], bank[2][:, 0:TR], ACT.Tanh, scale=0.5).then_inc(lp["tanh"], 1)
            take(eng, "down")
            eng.activation(y_sb[0][:], bank[6][0:TR, :], ACT.Copy, scale=l_entry[:, 1:2])\
               .then_inc(lp["y"], 1)

        def loop_dve(eng, r, x):
            take(eng, "load", 48)
            eng.tensor_copy(l_token[:], l_entry[:, 0:1]).then_inc(lp["token"], 1)
            take(eng, "tanh")
            eng.scalar_tensor_tensor(e_half[0][:, 0:TR], e_tanh[0][:, 0:TR], 1.0, bank[2][:, 0:TR], ALU.add,
                                     ALU.mult).then_inc(lp["half"], 1)
            take(eng, "half")
            eng.scalar_tensor_tensor(e_inner[0][:, 0:TR], e_half[0][:, 0:TR], 0.5, bank[3][:, 0:TR], ALU.mult,
                                     ALU.mult).then_inc(lp["inner"], 1)

        for queue, body in ((sp, loop_sp), (pool, loop_pool), (pe, loop_pe), (act, loop_act), (dve, loop_dve)):
            queue.wait(rounds_ready, *adds_over)
            queue.ops.append(loop(body))

        block = ctx.enter_context(nc.Block())
        block.sync(sp.play)
        block.tensor(pe.play)
        block.vector(dve.play)
        block.scalar(act.play)
        block.gpsimd(pool.play)


def lay_out(x, ctx_512, g_xattn, g_ffn, L0_xattn_Wq, L0_xattn_w_kc_q, L0_xattn_w_kc_kv, L0_xattn_W_qr, L0_xattn_W_kr,
            L0_xattn_Wo, L0_ffn_gate_w, L0_ffn_gu_w, L0_ffn_dp_w, L0_ffn_sh_gate_w, L0_ffn_sh_up_w, L0_ffn_sh_down_w,
            L0_ffn_sh_gate1_w):
    cut = lambda w: np.asarray(w).T.reshape(CJ, P, -1).transpose(1, 0, 2)
    arrays = {
        "x": np.asarray(x).reshape(B * S, C),
        "ctx": np.asarray(ctx_512),
        "g_xattn": np.asarray(g_xattn), "g_ffn": np.asarray(g_ffn),
        "w_q": np.asarray(L0_xattn_Wq).reshape(H, K, CJ, P).transpose(0, 3, 2, 1),
        "w_cq": np.asarray(L0_xattn_w_kc_q),
        "w_qr": np.asarray(L0_xattn_W_qr).transpose(2, 0, 1),
        "w_kr": np.asarray(L0_xattn_W_kr).transpose(2, 0, 1),
        "w_kv": np.asarray(L0_xattn_w_kc_kv).transpose(1, 0, 2),
        "w_o": np.asarray(L0_xattn_Wo).reshape(C, H, K).transpose(1, 2, 0),
        "token_w": cut(np.concatenate([np.asarray(w) for w in (L0_ffn_gate_w, L0_ffn_sh_gate1_w, L0_ffn_sh_gate_w,
                                                               L0_ffn_sh_up_w)])),
        "shared_out": np.asarray(L0_ffn_sh_down_w).T,
        "w_gu": np.asarray(L0_ffn_gu_w).reshape(E, 2 * I, CJ, P).transpose(0, 3, 2, 1),
        "w_dp": np.asarray(L0_ffn_dp_w).transpose(0, 2, 1),
    }
    arrays.update(shape_constants())
    return {k: np.ascontiguousarray(v) for k, v in arrays.items()}


def kernel(**inputs):
    import concourse.bacc as _bacc
    from concourse.bass_utils import run_bass_kernel_spmd as _run

    nc = _bacc.Bacc("TRN2", target_bir_lowering=False, num_devices=1)
    arrays = lay_out(**inputs)
    aps = {n: nc.dram_tensor(f"in_{n}", v.shape, mybir.dt.from_np(v.dtype), kind="ExternalInput").ap()
           for n, v in arrays.items()}
    out = nc.dram_tensor("out", [B * S + CAP, C], F32, kind="ExternalOutput").ap()
    build(nc, aps, out)
    r = _run(nc, [{f"in_{n}": v for n, v in arrays.items()}], core_ids=[0])
    return np.asarray(r.results[0]["out"])[:B * S].reshape(B, S, C)
```
